# Optimizing a Trainium2 kernel written in Bass

```python
import numpy as np
import jax
import jax.numpy as jnp

def _softmax(x, axis=-1):
    return jax.nn.softmax(x, axis=axis)

def _gelu(x):
    return jax.nn.gelu(x, approximate=True)

def _silu(x):
    return jax.nn.silu(x)

def _sigmoid(x):
    return jax.nn.sigmoid(x)

def _layernorm(x, axis=-1, eps=1e-05):
    m = jnp.mean(x, axis=axis, keepdims=True)
    v = jnp.var(x, axis=axis, keepdims=True)
    return (x - m) / jnp.sqrt(v + eps)

def _scatter_add(tgt, idx, src, axis=0):
    return tgt.at[idx].add(src)

def _segment_sum(src, seg, n):
    return jax.ops.segment_sum(src, seg, n)
kernel_name = 'mk_conv_seq_d2_conv_nchw384_r2_936206'

def setup_inputs(seed: int=0):
    np.random.seed(seed)
    _w = jnp.asarray

    def _rec_inputs():
        import jax
        import jax.numpy as jnp
        _gk = jax.random.key(seed)
        x = -4.65e-05 + 0.9999 * jax.random.normal(jax.random.fold_in(_gk, 1), (32, 192, 32, 32), jnp.float32)
        return x
    x = _rec_inputs()

    def _L0_conv_setup():
        import jax, jax.numpy as jnp
        import numpy as np
        DIM = 192
        HEADS = 12
        WS = 8
        SS = 4
        N = WS * WS
        HEAD_DIM = DIM // HEADS
        SCALE = HEAD_DIM ** (-0.5)
        MLP_HID = int(DIM * 4.0)

        def _relative_position_index():
            ch, cw = np.meshgrid(np.arange(WS), np.arange(WS), indexing='ij')
            coords = np.stack([ch, cw]).reshape(2, -1)
            rel = coords[:, :, None] - coords[:, None, :]
            rel = rel.transpose(1, 2, 0).astype(np.int64)
            rel[:, :, 0] += WS - 1
            rel[:, :, 1] += WS - 1
            rel[:, :, 0] *= 2 * WS - 1
            return jnp.asarray(rel.sum(-1))
        REL_IDX = _relative_position_index()

        def _shift_mask(H, W):
            img = np.zeros((H, W), dtype=np.float32)
            slices = (slice(0, -WS), slice(-WS, -SS), slice(-SS, None))
            cnt = 0
            for hs in slices:
                for ws_ in slices:
                    img[hs, ws_] = cnt
                    cnt += 1
            mw = img.reshape(H // WS, WS, W // WS, WS).transpose(0, 2, 1, 3).reshape(-1, N)
            diff = mw[:, None, :] - mw[:, :, None]
            return jnp.asarray(np.where(diff != 0, -10.0, 0.0).astype(np.float32))

        def _layernorm(x, g, b, eps=1e-05):
            mu = x.mean(-1, keepdims=True)
            var = ((x - mu) ** 2).mean(-1, keepdims=True)
            return (x - mu) * jax.lax.rsqrt(var + eps) * g + b
        key = jax.random.key(seed)
        ks = jax.random.split(key, 16)
        s = lambda fan_in: 1.0 / np.sqrt(fan_in)
        return {'x': jax.random.normal(ks[0], (32, DIM, 32, 32), jnp.float32), 'qkv_w': jax.random.normal(ks[1], (DIM, 3 * DIM), jnp.float32) * s(DIM), 'qkv_b': jnp.zeros((3 * DIM,), jnp.float32), 'proj_w': jax.random.normal(ks[2], (DIM, DIM), jnp.float32) * s(DIM), 'proj_b': jnp.zeros((DIM,), jnp.float32), 'rel_bias': jax.random.normal(ks[3], ((2 * WS - 1) ** 2, HEADS), jnp.float32) * 0.02, 'norm1_g': jnp.ones((DIM,), jnp.float32), 'norm1_b': jnp.zeros((DIM,), jnp.float32), 'norm2_g': jnp.ones((DIM,), jnp.float32), 'norm2_b': jnp.zeros((DIM,), jnp.float32), 'fc1_w': jax.random.normal(ks[4], (DIM, MLP_HID), jnp.float32) * s(DIM), 'fc1_b': jnp.zeros((MLP_HID,), jnp.float32), 'fc2_w': jax.random.normal(ks[5], (MLP_HID, DIM), jnp.float32) * s(MLP_HID), 'fc2_b': jnp.zeros((DIM,), jnp.float32)}
    _L0_conv_all = _L0_conv_setup()
    _L0_conv_in = {k: v for k, v in _L0_conv_all.items() if k in ('qkv_w', 'qkv_b', 'proj_w', 'proj_b', 'rel_bias', 'norm1_g', 'norm1_b', 'norm2_g', 'norm2_b', 'fc1_w', 'fc1_b', 'fc2_w', 'fc2_b')}
    del _L0_conv_all

    def _L1_conv_setup():
        import jax, jax.numpy as jnp
        import numpy as np
        DIM = 192
        WS = (8, 8)
        NH = 12
        HD = DIM // NH
        SHIFT = (WS[0] // 2, WS[1] // 2)
        EPS = 1e-05

        def layer_norm(x, gamma, beta):
            m = jnp.mean(x, axis=-1, keepdims=True)
            v = jnp.mean(jnp.square(x - m), axis=-1, keepdims=True)
            return (x - m) * jax.lax.rsqrt(v + EPS) * gamma + beta

        def window_attention(x, w_qkv, b_qkv, w_proj, b_proj):
            B, H, W, C = x.shape
            nh_h, nh_w = (H // WS[0], W // WS[1])
            L = WS[0] * WS[1]
            xw = x.reshape(B, nh_h, WS[0], nh_w, WS[1], C)
            xw = xw.transpose(0, 1, 3, 2, 4, 5).reshape(B * nh_h * nh_w, L, C)
            qkv = xw @ w_qkv + b_qkv
            qkv = qkv.reshape(-1, L, 3, NH, HD)
            q = qkv[:, :, 0].transpose(0, 2, 1, 3)
            k = qkv[:, :, 1].transpose(0, 2, 1, 3)
            v = qkv[:, :, 2].transpose(0, 2, 1, 3)
            attn = jnp.einsum('nhld,nhmd->nhlm', q, k) * HD ** (-0.5)
            attn = jax.nn.softmax(attn, axis=-1)
            out = jnp.einsum('nhlm,nhmd->nhld', attn, v)
            out = out.transpose(0, 2, 1, 3).reshape(-1, L, C)
            out = out @ w_proj + b_proj
            out = out.reshape(B, nh_h, nh_w, WS[0], WS[1], C)
            out = out.transpose(0, 1, 3, 2, 4, 5).reshape(B, H, W, C)
            return out

        def swin_block(x, gamma1, beta1, w_qkv, b_qkv, w_proj, b_proj, gamma2, beta2, w_fc1, b_fc1, w_fc2, b_fc2):
            x = x.transpose(0, 2, 3, 1)
            shortcut = x
            x = layer_norm(x, gamma1, beta1)
            x = jnp.roll(x, shift=(-SHIFT[0], -SHIFT[1]), axis=(1, 2))
            x = window_attention(x, w_qkv, b_qkv, w_proj, b_proj)
            x = jnp.roll(x, shift=(SHIFT[0], SHIFT[1]), axis=(1, 2))
            x = shortcut + x
            shortcut = x
            x = layer_norm(x, gamma2, beta2)
            x = jax.nn.gelu(x @ w_fc1 + b_fc1, approximate=False) @ w_fc2 + b_fc2
            x = shortcut + x
            return x.transpose(0, 3, 1, 2)
        key = jax.random.key(seed)
        ks = jax.random.split(key, 8)
        B, C, H, W = (16, DIM, 32, 32)
        hidden = 4 * DIM
        s = 0.02
        return {'x': jax.random.normal(ks[0], (B, C, H, W), jnp.float32), 'gamma1': jnp.ones((DIM,), jnp.float32), 'beta1': jnp.zeros((DIM,), jnp.float32), 'w_qkv': jax.random.normal(ks[1], (DIM, 3 * DIM), jnp.float32) * s, 'b_qkv': jnp.zeros((3 * DIM,), jnp.float32), 'w_proj': jax.random.normal(ks[2], (DIM, DIM), jnp.float32) * s, 'b_proj': jnp.zeros((DIM,), jnp.float32), 'gamma2': jnp.ones((DIM,), jnp.float32), 'beta2': jnp.zeros((DIM,), jnp.float32), 'w_fc1': jax.random.normal(ks[3], (DIM, hidden), jnp.float32) * s, 'b_fc1': jnp.zeros((hidden,), jnp.float32), 'w_fc2': jax.random.normal(ks[4], (hidden, DIM), jnp.float32) * s, 'b_fc2': jnp.zeros((DIM,), jnp.float32)}
    _L1_conv_all = _L1_conv_setup()
    _L1_conv_in = {k: v for k, v in _L1_conv_all.items() if k in ('gamma1', 'beta1', 'w_qkv', 'b_qkv', 'w_proj', 'b_proj', 'gamma2', 'beta2', 'w_fc1', 'b_fc1', 'w_fc2', 'b_fc2')}
    del _L1_conv_all
    return {'x': x, 'L0_conv_qkv_w': _L0_conv_in['qkv_w'], 'L0_conv_qkv_b': _L0_conv_in['qkv_b'], 'L0_conv_proj_w': _L0_conv_in['proj_w'], 'L0_conv_proj_b': _L0_conv_in['proj_b'], 'L0_conv_rel_bias': _L0_conv_in['rel_bias'], 'L0_conv_norm1_g': _L0_conv_in['norm1_g'], 'L0_conv_norm1_b': _L0_conv_in['norm1_b'], 'L0_conv_norm2_g': _L0_conv_in['norm2_g'], 'L0_conv_norm2_b': _L0_conv_in['norm2_b'], 'L0_conv_fc1_w': _L0_conv_in['fc1_w'], 'L0_conv_fc1_b': _L0_conv_in['fc1_b'], 'L0_conv_fc2_w': _L0_conv_in['fc2_w'], 'L0_conv_fc2_b': _L0_conv_in['fc2_b'], 'L1_conv_gamma1': _L1_conv_in['gamma1'], 'L1_conv_beta1': _L1_conv_in['beta1'], 'L1_conv_w_qkv': _L1_conv_in['w_qkv'], 'L1_conv_b_qkv': _L1_conv_in['b_qkv'], 'L1_conv_w_proj': _L1_conv_in['w_proj'], 'L1_conv_b_proj': _L1_conv_in['b_proj'], 'L1_conv_gamma2': _L1_conv_in['gamma2'], 'L1_conv_beta2': _L1_conv_in['beta2'], 'L1_conv_w_fc1': _L1_conv_in['w_fc1'], 'L1_conv_b_fc1': _L1_conv_in['b_fc1'], 'L1_conv_w_fc2': _L1_conv_in['w_fc2'], 'L1_conv_b_fc2': _L1_conv_in['b_fc2']}

def reference(x, L0_conv_qkv_w, L0_conv_qkv_b, L0_conv_proj_w, L0_conv_proj_b, L0_conv_rel_bias, L0_conv_norm1_g, L0_conv_norm1_b, L0_conv_norm2_g, L0_conv_norm2_b, L0_conv_fc1_w, L0_conv_fc1_b, L0_conv_fc2_w, L0_conv_fc2_b, L1_conv_gamma1, L1_conv_beta1, L1_conv_w_qkv, L1_conv_b_qkv, L1_conv_w_proj, L1_conv_b_proj, L1_conv_gamma2, L1_conv_beta2, L1_conv_w_fc1, L1_conv_b_fc1, L1_conv_w_fc2, L1_conv_b_fc2):
    import jax
    import jax.numpy as jnp

    def _L0_conv_ref(x, qkv_w, qkv_b, proj_w, proj_b, rel_bias, norm1_g, norm1_b, norm2_g, norm2_b, fc1_w, fc1_b, fc2_w, fc2_b):
        import jax, jax.numpy as jnp
        import numpy as np
        DIM = 192
        HEADS = 12
        WS = 8
        SS = 4
        N = WS * WS
        HEAD_DIM = DIM // HEADS
        SCALE = HEAD_DIM ** (-0.5)
        MLP_HID = int(DIM * 4.0)

        def _relative_position_index():
            ch, cw = np.meshgrid(np.arange(WS), np.arange(WS), indexing='ij')
            coords = np.stack([ch, cw]).reshape(2, -1)
            rel = coords[:, :, None] - coords[:, None, :]
            rel = rel.transpose(1, 2, 0).astype(np.int64)
            rel[:, :, 0] += WS - 1
            rel[:, :, 1] += WS - 1
            rel[:, :, 0] *= 2 * WS - 1
            return jnp.asarray(rel.sum(-1))
        REL_IDX = _relative_position_index()

        def _shift_mask(H, W):
            img = np.zeros((H, W), dtype=np.float32)
            slices = (slice(0, -WS), slice(-WS, -SS), slice(-SS, None))
            cnt = 0
            for hs in slices:
                for ws_ in slices:
                    img[hs, ws_] = cnt
                    cnt += 1
            mw = img.reshape(H // WS, WS, W // WS, WS).transpose(0, 2, 1, 3).reshape(-1, N)
            diff = mw[:, None, :] - mw[:, :, None]
            return jnp.asarray(np.where(diff != 0, -10.0, 0.0).astype(np.float32))

        def _layernorm(x, g, b, eps=1e-05):
            mu = x.mean(-1, keepdims=True)
            var = ((x - mu) ** 2).mean(-1, keepdims=True)
            return (x - mu) * jax.lax.rsqrt(var + eps) * g + b
        B, C, H, W = x.shape
        x = x.transpose(0, 2, 3, 1)
        shortcut = x
        xn = _layernorm(x, norm1_g, norm1_b)
        xs = jnp.roll(xn, shift=(-SS, -SS), axis=(1, 2))
        nWh, nWw = (H // WS, W // WS)
        nW = nWh * nWw
        xw = xs.reshape(B, nWh, WS, nWw, WS, C).transpose(0, 1, 3, 2, 4, 5).reshape(B * nW, N, C)
        qkv = (xw @ qkv_w + qkv_b).reshape(B * nW, N, 3, HEADS, HEAD_DIM).transpose(2, 0, 3, 1, 4)
        q, k, v = (qkv[0] * SCALE, qkv[1], qkv[2])
        attn = jnp.einsum('bhnd,bhmd->bhnm', q, k)
        bias = rel_bias[REL_IDX.reshape(-1)].reshape(N, N, HEADS).transpose(2, 0, 1)
        attn = attn + bias[None]
        mask = _shift_mask(H, W)
        attn = attn.reshape(B, nW, HEADS, N, N) + mask[None, :, None]
        attn = attn.reshape(B * nW, HEADS, N, N)
        attn = jax.nn.softmax(attn, axis=-1)
        out = jnp.einsum('bhnm,bhmd->bhnd', attn, v).transpose(0, 2, 1, 3).reshape(B * nW, N, C)
        out = out @ proj_w + proj_b
        xs = out.reshape(B, nWh, nWw, WS, WS, C).transpose(0, 1, 3, 2, 4, 5).reshape(B, H, W, C)
        x = shortcut + jnp.roll(xs, shift=(SS, SS), axis=(1, 2))
        h = _layernorm(x, norm2_g, norm2_b)
        h = jax.nn.gelu(h @ fc1_w + fc1_b, approximate=False)
        x = x + (h @ fc2_w + fc2_b)
        return x.transpose(0, 3, 1, 2)

    def _L1_conv_ref(x, gamma1, beta1, w_qkv, b_qkv, w_proj, b_proj, gamma2, beta2, w_fc1, b_fc1, w_fc2, b_fc2):
        import jax, jax.numpy as jnp
        import numpy as np
        DIM = 192
        WS = (8, 8)
        NH = 12
        HD = DIM // NH
        SHIFT = (WS[0] // 2, WS[1] // 2)
        EPS = 1e-05

        def layer_norm(x, gamma, beta):
            m = jnp.mean(x, axis=-1, keepdims=True)
            v = jnp.mean(jnp.square(x - m), axis=-1, keepdims=True)
            return (x - m) * jax.lax.rsqrt(v + EPS) * gamma + beta

        def window_attention(x, w_qkv, b_qkv, w_proj, b_proj):
            B, H, W, C = x.shape
            nh_h, nh_w = (H // WS[0], W // WS[1])
            L = WS[0] * WS[1]
            xw = x.reshape(B, nh_h, WS[0], nh_w, WS[1], C)
            xw = xw.transpose(0, 1, 3, 2, 4, 5).reshape(B * nh_h * nh_w, L, C)
            qkv = xw @ w_qkv + b_qkv
            qkv = qkv.reshape(-1, L, 3, NH, HD)
            q = qkv[:, :, 0].transpose(0, 2, 1, 3)
            k = qkv[:, :, 1].transpose(0, 2, 1, 3)
            v = qkv[:, :, 2].transpose(0, 2, 1, 3)
            attn = jnp.einsum('nhld,nhmd->nhlm', q, k) * HD ** (-0.5)
            attn = jax.nn.softmax(attn, axis=-1)
            out = jnp.einsum('nhlm,nhmd->nhld', attn, v)
            out = out.transpose(0, 2, 1, 3).reshape(-1, L, C)
            out = out @ w_proj + b_proj
            out = out.reshape(B, nh_h, nh_w, WS[0], WS[1], C)
            out = out.transpose(0, 1, 3, 2, 4, 5).reshape(B, H, W, C)
            return out

        def swin_block(x, gamma1, beta1, w_qkv, b_qkv, w_proj, b_proj, gamma2, beta2, w_fc1, b_fc1, w_fc2, b_fc2):
            x = x.transpose(0, 2, 3, 1)
            shortcut = x
            x = layer_norm(x, gamma1, beta1)
            x = jnp.roll(x, shift=(-SHIFT[0], -SHIFT[1]), axis=(1, 2))
            x = window_attention(x, w_qkv, b_qkv, w_proj, b_proj)
            x = jnp.roll(x, shift=(SHIFT[0], SHIFT[1]), axis=(1, 2))
            x = shortcut + x
            shortcut = x
            x = layer_norm(x, gamma2, beta2)
            x = jax.nn.gelu(x @ w_fc1 + b_fc1, approximate=False) @ w_fc2 + b_fc2
            x = shortcut + x
            return x.transpose(0, 3, 1, 2)
        return swin_block(x, gamma1, beta1, w_qkv, b_qkv, w_proj, b_proj, gamma2, beta2, w_fc1, b_fc1, w_fc2, b_fc2)

    def _gn(v, G=32, eps=1e-05):
        B_, C_, H_, W_ = v.shape
        g = v.reshape(B_, G, C_ // G, H_, W_)
        m = jnp.mean(g, axis=(2, 3, 4), keepdims=True)
        s = jnp.var(g, axis=(2, 3, 4), keepdims=True)
        return ((g - m) / jnp.sqrt(s + eps)).reshape(v.shape)

    def _ln_c(v, eps=1e-06):
        m = jnp.mean(v, axis=1, keepdims=True)
        s = jnp.var(v, axis=1, keepdims=True)
        return (v - m) / jnp.sqrt(s + eps)

    def _ln_t(v, eps=1e-05):
        m = jnp.mean(v, axis=-1, keepdims=True)
        s = jnp.var(v, axis=-1, keepdims=True)
        return (v - m) / jnp.sqrt(s + eps)

    def _to_tokens(v):
        B_, C_, H_, W_ = v.shape
        return v.reshape(B_, C_, H_ * W_).transpose(0, 2, 1)

    def _from_tokens(t, like):
        B_, C_, H_, W_ = like.shape
        return t.transpose(0, 2, 1).reshape(B_, C_, H_, W_)
    x = _L0_conv_ref(x, L0_conv_qkv_w, L0_conv_qkv_b, L0_conv_proj_w, L0_conv_proj_b, L0_conv_rel_bias, L0_conv_norm1_g, L0_conv_norm1_b, L0_conv_norm2_g, L0_conv_norm2_b, L0_conv_fc1_w, L0_conv_fc1_b, L0_conv_fc2_w, L0_conv_fc2_b)
    x = _L1_conv_ref(x, L1_conv_gamma1, L1_conv_beta1, L1_conv_w_qkv, L1_conv_b_qkv, L1_conv_w_proj, L1_conv_b_proj, L1_conv_gamma2, L1_conv_beta2, L1_conv_w_fc1, L1_conv_b_fc1, L1_conv_w_fc2, L1_conv_b_fc2)
    return x

_drawn_inputs = setup_inputs


def setup_inputs(seed=0):
    import zlib

    import numpy as np

    out = dict(_drawn_inputs(seed))
    spreads = {'L0_conv_qkv_b': (0.0, 0.1),
     'L0_conv_proj_b': (0.0, 0.1),
     'L0_conv_norm1_g': (1.0, 0.2),
     'L0_conv_norm1_b': (0.0, 0.1),
     'L0_conv_norm2_g': (1.0, 0.2),
     'L0_conv_norm2_b': (0.0, 0.1),
     'L0_conv_fc1_b': (0.0, 0.1),
     'L0_conv_fc2_b': (0.0, 0.1),
     'L1_conv_gamma1': (1.0, 0.6),
     'L1_conv_beta1': (0.0, 0.8),
     'L1_conv_b_qkv': (0.0, 0.371),
     'L1_conv_b_proj': (0.0, 0.1),
     'L1_conv_gamma2': (1.0, 0.6),
     'L1_conv_beta2': (0.0, 0.8),
     'L1_conv_b_fc1': (0.0, 0.366),
     'L1_conv_b_fc2': (0.0, 0.1)}
    factors = {'L0_conv_rel_bias': 8.0}
    for name, (base, spread) in spreads.items():
        noise = np.random.default_rng([zlib.crc32(name.encode()), seed]).standard_normal(out[name].shape)
        drawn = base * np.exp(spread * noise) if base else spread * noise
        out[name] = jnp.asarray(drawn.astype(out[name].dtype))
    for name, factor in factors.items():
        out[name] = (out[name] * factor).astype(out[name].dtype)
    return out
```

```python
from contextlib import ExitStack

import concourse.bass as bass
from concourse import mybir

F32 = mybir.dt.float32
F16 = mybir.dt.float16
BF16 = mybir.dt.bfloat16
ALU = mybir.AluOpType
ACT = mybir.ActivationFunctionType
AX = mybir.AxisListType

IMAGES, C, SIDE = 32, 192, 32
HEADS, HD = 12, 16
PAIRS = HEADS // 2
WS, SHIFT = 8, 4
WIN = WS * WS
TOK = 2 * WIN
TILES = SIDE * SIDE // TOK
LAYERS = 2
STEPS = LAYERS * TILES
GROUP = 4
PHASES = STEPS // GROUP
HID = 4 * C
HC = HID // 128
CB = 64
WSCALE = 64.0
UNSCALE = 1.0 / WSCALE
QSCALE = HD ** -0.5
VW = HD + 1
CREDIT = 4
FIRST, LAST = 3, 3 + STEPS
EPS = 1e-5


def visit(n):
    layer, group = ((1, 1), (0, 1), (1, 0), (0, 0))[n // GROUP % PHASES]
    return layer, group * GROUP + n % GROUP


def visit_in_layer(n):
    layer, _ = visit(n)
    return (n + (0 if layer else GROUP)) // (2 * GROUP) * GROUP + n % GROUP


def mlp_phase(s):
    return (s - FIRST) // GROUP - 1, (s - FIRST) % GROUP


def window_pieces(t):
    i, jp = t // 2, t % 2
    rows = [(0, WS, WS * i + SHIFT)] if i < 3 else [(0, SHIFT, SIDE - SHIFT), (SHIFT, SHIFT, 0)]
    cols = [(0, 2, 0, WS, SHIFT)] if jp == 0 else [
        (0, 1, 0, WS, 2 * WS + SHIFT), (1, 1, 0, SHIFT, SIDE - SHIFT), (1, 1, SHIFT, SHIFT, 0)]
    return [(w0, nw, r0, nr, c0, nc, row, col) for r0, nr, row in rows for w0, nw, c0, nc, col in cols]


def box_pairs(t, tile_view, image_view):
    tv = tile_view.rearrange("p k (w r c) -> p k w r c", w=2, r=WS)
    iv = image_view.rearrange("p k (r c) -> p k r c", r=SIDE)
    out = []
    for w0, nw, r0, nr, c0, nc, row, col in window_pieces(t):
        if nw == 2:
            for k in range(2):
                out.append((tv[:, k, :, r0:r0 + nr, :],
                            iv[:, k, row:row + nr, col:col + 2 * WS].rearrange("p r (w c) -> p w r c", w=2)))
        else:
            out.append((tv[:, :, w0, r0:r0 + nr, c0:c0 + nc], iv[:, :, row:row + nr, col:col + nc]))
    return out


def swin_program(nc, x, layers, rel_bias, ident_in, mask_in, out):
    H2 = C // 2
    with ExitStack() as ctx:
        def sb(name, shape, dt):
            return ctx.enter_context(nc.sbuf_tensor(name, shape, dt))

        def sem(name):
            return ctx.enter_context(nc.semaphore(name))

        banks = [ctx.enter_context(nc.psum_tensor(f"bank{i}", [128, 512], F32)) for i in range(4)]
        ps_s = ctx.enter_context(nc.psum_tensor("ps_s", [128, 2, 512], F32))
        ps_t = ctx.enter_context(nc.psum_tensor("ps_t", [128, 2, 512], F32))
        ps_tr, ps_o, ps_qk, ps_v = banks
        ps_tr16 = ps_tr[:, :].bitcast(F16)
        ps_o16 = ps_o[:, :].bitcast(F16)
        ps_t16 = [ps_t[:, i, :].bitcast(F16) for i in range(2)]

        ident = sb("ident", [128, 128], F32)
        ident16 = sb("ident16", [128, 128], F16)
        neg_ident = sb("neg_ident", [128, 128], BF16)
        ones16 = sb("ones16", [128, 128], F16)
        ones_row = sb("ones_row", [1, 128], F32)
        mask = sb("mask", [128, 4, WIN], F32)
        rel = sb("rel", [128, WIN, HEADS], F32)
        rel_t = sb("rel_t", [128, 2, PAIRS, WIN], F32)
        rel_m = sb("rel_m", [128, 2, PAIRS, WIN], F32)
        bias_tab = sb("bias_tab", [128, 4, 2, 2, PAIRS, WIN], F16)
        stage = sb("stage", [128, 2, HID], F32)
        scaled = sb("scaled", [128, 2, HID], F32)
        cols = sb("cols", [128, LAYERS, 4, 2], F32)
        vcol = sb("vcol", [128, 2], F32)
        row = sb("row", [1, 5 * C], F32)
        rowsum = sb("rowsum", [1, 2 * C], F32)
        w_qkv = [sb(f"w_qkv{l}", [128, 4, 3 * C], F16) for l in range(LAYERS)]
        w_proj = [sb(f"w_proj{l}", [128, 4, C], F16) for l in range(LAYERS)]
        w_fc1 = [sb(f"w_fc1{l}", [128, 4, HID], F16) for l in range(LAYERS)]
        w_fc2 = [sb(f"w_fc2{l}", [128, 2, HC, C], F16) for l in range(LAYERS)]
        b_qk = [sb(f"b_qk{l}", [128, 2 * C], F16) for l in range(LAYERS)]
        b_proj = [sb(f"b_proj{l}", [128, C], F32) for l in range(LAYERS)]
        b_fc1 = [sb(f"b_fc1{l}", [128, HC], F32) for l in range(LAYERS)]
        b_fc2 = [sb(f"b_fc2{l}", [128, C], F32) for l in range(LAYERS)]

        x_img = sb("x_img", [H2, 2, SIDE * SIDE], F32)
        x_win = sb("x_win", [H2, 2, SIDE * SIDE], F32)
        y_img = sb("y_img", [H2, 2, SIDE * SIDE], F32)
        x_new = sb("x_new", [128, GROUP, C], F32)
        x_mid = sb("x_mid", [128, GROUP, C], F32)
        x_tok = sb("x_tok", [128, TILES, C], F32)
        bn6 = sb("bn6", [128, 2, 2, 6], F32)
        mv = sb("mv", [128, 2, 2, 2], F32)
        nmean = sb("nmean", [128, 2, 2], F32)
        vare = sb("vare", [128, 2, 2], F32)
        rstd = sb("rstd", [128, 2, 2], F32)
        half = sb("half", [128, 1], F32)
        xn = sb("xn", [128, 2, 2, C], F32)
        xs = sb("xs", [128, 2, 2, 2, C], F16)
        xt = sb("xt", [128, 2, 3, TOK], F16)
        ht = sb("ht", [128, 2, 3, GROUP * TOK], F16)
        qk = sb("qk", [128, 2, 2 * HEADS, 4, HD], F16)
        qt = sb("qt", [128, 2, PAIRS, TOK], F16)
        kt = sb("kt", [128, 2, PAIRS, TOK], F16)
        v_blk = sb("v_blk", [128, 2, 2, PAIRS, 2, 2, VW], F16)
        smax = sb("smax", [128, 2, 2, PAIRS], BF16)
        p_tok = sb("p_tok", [128, 2, PAIRS, 2, WIN], F32)
        pt = sb("pt", [128, 2, 2, PAIRS, TOK], F16)
        o_raw = sb("o_raw", [128, 2, HEADS, VW], F32)
        o_inv = sb("o_inv", [128, 2, HEADS], F32)
        o_tok = sb("o_tok", [128, 2, C], F32)
        os = sb("os", [128, 2, 2, C], F16)
        ot = sb("ot", [128, 2, 3, TOK], F16)
        hid = sb("hid", [128, 2, GROUP * TOK], F32)
        hid16 = sb("hid16", [128, 2, HC, GROUP * TOK], F16)

        const_in = [sem(f"const_in{i}") for i in range(3)]
        norm_in = [sem(f"norm_in{l}") for l in range(LAYERS)]
        w_in = [sem(f"w_in{j}") for j in range(4 * LAYERS)]
        folded = sem("folded")
        made = sem("made")
        dve_chain = sem("dve_chain")
        tables = sem("tables")

        COUNT = {name: STEPS for name in (
            "bn1a bn1 ln1a ln1b ln1 bias1 hi1 lo1 tr1 xt_done qk_mm v_mm qk_hi qk_lo v_hi v_lo tqk q_evac "
            "k_evac s_mm max_done shift exp_done tp p_hi p_lo pv o_evac inv_done o_norm o_hi o_lo to ot_done "
            "pr resid1 bn2a bn2 ln2a ln2b ln2 bias2 hi2 lo2 tr2 ht_done fc2 resid2").split()}
        AHEAD = dict.fromkeys(COUNT, GROUP)
        COUNT |= {name: PHASES * HC for name in ("fc1", "gelu", "h_hi", "h_lo")}
        AHEAD |= {name: HC for name in ("fc1", "gelu", "h_hi", "h_lo")}
        COUNT |= {name: TILES for name in ("xtr", "x_in", "otr", "y_ready")}
        AHEAD |= {name: 0 for name in ("xtr", "x_in", "otr", "y_ready")}
        S = {name: sem(name) for name in COUNT}
        x_loaded = sem("x_loaded")
        x_ordered = sem("x_ordered")
        y_stored = sem("y_stored")

        def when(eng, it, name, n):
            eng.wait_ge(S[name], it * COUNT[name] + (n + 1 + AHEAD[name] + CREDIT))

        def stream(n, which):
            layer, t = visit(n)
            return x_tok[:, t, :] if layer else (x_new, x_mid)[which][:, t % GROUP, :]

        def run(eng, slot):
            for s in range(-2 * GROUP, FIRST):
                slot(0, s, lambda n: n >= -GROUP)
            with eng.Fori(0, IMAGES) as it:
                for s in range(FIRST, LAST):
                    slot(it, s, lambda n: True)
            for s in range(LAST, STEPS + GROUP + 7):
                slot(IMAGES - 1, s, lambda n: n < STEPS + GROUP)

        def v_places(n, par, w, part):
            src = ps_v[w * WIN:(w + 1) * WIN, 0:C].rearrange("p (g a d) -> p g a d", a=2, d=HD)[:, :, par]
            return src, v_blk[par * 64:par * 64 + 64, n % 2, part, :, par, w, 0:HD]

        block = ctx.enter_context(nc.Block())
        A, B = slice(CB, C), slice(0, CB)

        @block.sync
        def _(sp):
            sp.sem_inc(y_stored, 16)
            sp.dma_start(x_img[:, :, :], x[0].rearrange("(k p) h w -> p k (h w)", k=2)).then_inc(x_loaded, 16)
            sp.dma_start(ident[:, :], ident_in).then_inc(const_in[0], 16)
            sp.dma_start(mask[:, :, :], mask_in).then_inc(const_in[1], 16)
            span = 2 * WS - 1
            for w in range(2):
                for qr in range(WS):
                    src = bass.AP(tensor=rel_bias.tensor, offset=rel_bias.offset + qr * span * HEADS,
                                  ap=[[HEADS, WS], [span * HEADS, WS], [HEADS, WS], [1, HEADS]])
                    p0 = w * WIN + qr * WS
                    sp.dma_start(rel[p0:p0 + WS, :, :].rearrange("p (a b) h -> p a b h", a=WS), src)\
                        .then_inc(const_in[2], 16)
            for l, L in enumerate(layers):
                for i, name in enumerate(("g1", "b1", "g2", "b2")):
                    v = L[name].rearrange("(c a) -> c a", a=1)
                    sp.dma_start(cols[:, l, i, 0:1], v[A, :]).then_inc(norm_in[l], 16)
                    sp.dma_start(cols[0:CB, l, i, 1:2], v[B, :]).then_inc(norm_in[l], 16)
                    sp.dma_start(cols[CB:128, l, i, 1:2], v[B, :]).then_inc(norm_in[l], 16)
            for l, L in enumerate(layers):
                for k, (name, n) in enumerate((("wqkv", 3 * C), ("wproj", C), ("wfc1", HID), ("wfc2", 0))):
                    j = 4 * l + k
                    if j:
                        sp.wait_ge(made, 1 + j)
                    if k == 0:
                        for i, (bias, m) in enumerate((("bqkv", 3 * C), ("bproj", C), ("bfc2", C))):
                            o = (0, 3 * C, 4 * C)[i]
                            sp.dma_start(row[:, o:o + m], L[bias].rearrange("(a c) -> a c", a=1)).then_inc(w_in[j], 16)
                        bv = L["bqkv"].rearrange("(c a) -> c a", a=1)
                        sp.dma_start(vcol[:, 0:1], bv[2 * C + CB:3 * C, :]).then_inc(w_in[j], 16)
                        sp.dma_start(vcol[0:CB, 1:2], bv[2 * C:2 * C + CB, :]).then_inc(w_in[j], 16)
                    if k == 2:
                        sp.dma_start(b_fc1[l][:, :], L["bfc1"].rearrange("(m p) -> p m", p=128),
                                     allow_slow_non_contiguous=True).then_inc(w_in[j], 16)
                    if n:
                        sp.dma_start(stage[:, 0, 0:n], L[name][A, :]).then_inc(w_in[j], 16)
                        sp.dma_start(stage[0:CB, 1, 0:n], L[name][B, :]).then_inc(w_in[j], 16)
                        sp.dma_start(stage[CB:128, 1, 0:n], L[name][B, :]).then_inc(w_in[j], 16)
                    else:
                        sp.dma_start(stage[:, :, :].rearrange("p a n -> p (a n)")[:, 0:HC * C]
                                     .rearrange("p (m c) -> p m c", m=HC),
                                     L[name].rearrange("(m p) c -> p m c", p=128)).then_inc(w_in[j], 16)
            def next_image(it):
                sp.wait_ge(x_ordered, it + 1)
                following = (it + 1) % IMAGES
                sp.dma_start(x_img[:, :, :], x[following if isinstance(it, int) else sp.snap(following)]
                             .rearrange("(k p) h w -> p k (h w)", k=2)).then_inc(x_loaded, 16)

            def store(image):
                sp.dma_start(out[image].rearrange("(k p) h w -> p k (h w)", k=2), y_img[:, :, :])\
                    .then_inc(y_stored, 16)

            next_image(0)
            with sp.Fori(1, IMAGES) as it:
                next_image(it)
                when(sp, it, "y_ready", GROUP - 1)
                store(sp.snap(it - 1))
            when(sp, IMAGES - 1, "y_ready", TILES + GROUP - 1)
            store(IMAGES - 1)
            sp.wait_ge(y_stored, 16 * (IMAGES + 1))
            sp.wait_ge(x_loaded, 16 * (IMAGES + 1))

        W_DMAS = [8, 3, 4, 1]

        @block.tensor
        def _(pe):
            mm = nc.tensor.matmul
            for name in ("tr1", "qk_mm", "v_mm", "tqk", "s_mm", "shift", "tp", "pv", "to", "pr", "tr2", "fc1", "fc2",
                         "xtr", "otr"):
                pe.sem_inc(S[name], CREDIT)

            for l in range(LAYERS):
                sA1, sB1 = cols[:, l, 1, 0:1], cols[0:CB, l, 1, 1:2]
                sA2, sB2 = cols[:, l, 3, 0:1], cols[0:CB, l, 3, 1:2]
                pe.wait_ge(norm_in[l], 16 * 12)
                pe.wait_ge(w_in[4 * l], 16 * W_DMAS[0])
                pe.wait_ge(made, 1 + 4 * l)
                mm(ps_qk[0:1, 0:2 * C], sA1, stage[:, 0, 0:2 * C], start=True, stop=False)
                mm(ps_qk[0:1, 0:2 * C], sB1, stage[0:CB, 1, 0:2 * C], start=False, stop=True)
                for j, cs in enumerate((slice(2 * C + CB, 3 * C), slice(2 * C, 2 * C + CB))):
                    m = cs.stop - cs.start
                    mm(ps_v[0:m, j:j + 1], stage[:, 0, cs], sA1, start=True, stop=False)
                    last = mm(ps_v[0:m, j:j + 1], stage[0:CB, 1, cs], sB1, start=False, stop=True)
                last.then_inc(folded, 1)
                pe.wait_ge(w_in[4 * l + 1], 16 * W_DMAS[1])
                pe.wait_ge(made, 2 + 4 * l)
                mm(ps_o[0:1, 0:C], vcol[:, 0:1], stage[:, 0, 0:C], start=True, stop=False)
                mm(ps_o[0:1, 0:C], vcol[0:CB, 1:2], stage[0:CB, 1, 0:C], start=False, stop=True).then_inc(folded, 1)
                pe.wait_ge(w_in[4 * l + 2], 16 * W_DMAS[2])
                for m in range(HC):
                    cs = slice(m * 128, (m + 1) * 128)
                    mm(ps_s[:, 0, m:m + 1], stage[:, 0, cs], sA2, start=True, stop=False)
                    last = mm(ps_s[:, 0, m:m + 1], stage[0:CB, 1, cs], sB2, start=False, stop=True)
                last.then_inc(folded, 1)
                pe.wait_ge(made, 3 + 4 * l)
                mm(ps_t[:, 0, 0:2 * C], ones_row[:, :], rowsum[:, :], start=True, stop=True).then_inc(folded, 1)
            pe.wait_ge(made, 1 + 4 * LAYERS)
            pe.wait_ge(tables, 1)


            def slot(it, s, live):
                def ge(name, n):
                    when(pe, it, name, n)

                def take_tr(reader, n):
                    ge(*tr_reader)
                    tr_reader[:] = [reader, n]

                def contract(dst, w, lhs_tile, n0, n1, first=True):
                    for i, (blk, part) in enumerate(((0, 0), (2, 0), (0, 1), (1, 2), (1, 3))):
                        last = mm(dst, lhs_tile(blk), w[:, part, n0:n1], start=(first and i == 0), stop=(i == 4))
                    return last

                def transpose3(dst16, src):
                    nc.tensor.transpose(dst16[:, 0:TOK], src[:, 0, A], ident16[:, :])
                    for part in range(2):
                        nc.tensor.transpose(dst16[part * CB:(part + 1) * CB, TOK:2 * TOK], src[:, part, B], ident16[:, :])
                    return nc.tensor.transpose(dst16[:, 2 * TOK:3 * TOK], src[:, 1, A], ident16[:, :])

                def x_transpose(n):
                    layer, t = visit(n)
                    take_tr("x_in", visit_in_layer(n))
                    if t == 0:
                        pe.wait_ge(x_ordered, 1 if n < 0 else it + 2)
                    for k in range(2):
                        last = nc.tensor.transpose(ps_tr[:, k * H2:(k + 1) * H2], x_win[:, k, t * TOK:(t + 1) * TOK],
                                                   ident[0:H2, 0:H2])
                    last.then_inc(S["xtr"], 1)

                def norm1_transpose(n):
                    take_tr("xt_done", n)
                    ge("lo1", n)
                    transpose3(ps_tr16, xs[:, 0, n % 2]).then_inc(S["tr1"], 1)

                def qk_product(n):
                    layer, t = visit(n)
                    ge("resid1", n - 3)
                    ge("xt_done", n)
                    mm(ps_qk[:, 0:2 * C], ones16[:, :], b_qk[layer][:, :], start=True, stop=False)
                    contract(ps_qk[:, 0:2 * C], w_qkv[layer], lambda b: xt[:, n % 2, b, :], 0, 2 * C,
                             first=False).then_inc(S["qk_mm"], 1)

                def v_product(n):
                    layer, t = visit(n)
                    p, place = mlp_phase(n - 1)
                    if place == 1 and p >= -1:
                        ge("resid2", p * GROUP + 1)
                    else:
                        ge("v_lo", n - 1)
                    contract(ps_v[:, 0:C], w_qkv[layer], lambda b: xt[:, n % 2, b, :], 2 * C, 3 * C)\
                        .then_inc(S["v_mm"], 1)

                def qk_transpose(n):
                    ge("p_lo", n - 1)
                    ge("qk_lo", n)
                    for qk_half in range(2):
                        for g in range(PAIRS):
                            h = qk_half * HEADS + 2 * g
                            last = nc.tensor.transpose(ps_t16[qk_half][:, g * TOK:(g + 1) * TOK],
                                                       qk[:, n % 2, h:h + 2].rearrange("p h s d -> p (h s d)"),
                                                       ident16[:, :])
                    last.then_inc(S["tqk"], 1)

                def scores(n):
                    layer, t = visit(n)
                    p, place = mlp_phase(n)
                    if place == 0 and p >= -1:
                        ge("gelu", p * HC + HC - 1)
                    ge("exp_done", n - 1)
                    ge("q_evac", n)
                    ge("k_evac", n)
                    if layer == 0:
                        kind = 2 * (t // 2 == 3) + t % 2
                        for par in range(2):
                            for part in range(2):
                                mm(ps_s[:, par, 0:PAIRS * WIN], ident16[:, :], bias_tab[:, kind, part, par, :, :],
                                   start=(part == 0), stop=False, skip_group_check=True)
                    else:
                        pe.nop(nofuse=True)
                    for g in range(PAIRS):
                        for w in range(2):
                            for par in range(2):
                                rows = slice(par * 64, par * 64 + 64)
                                tok = slice(w * WIN, (w + 1) * WIN)
                                last = mm(ps_s[w * WIN:(w + 1) * WIN, par, g * WIN:(g + 1) * WIN],
                                          qt[rows, n % 2, g, tok], kt[rows, n % 2, g, tok],
                                          start=(layer == 1 and g == 0), stop=False, skip_group_check=True)
                    last.then_inc(S["s_mm"], 1)

                def shift_scores(n):
                    ge("max_done", n)
                    for par in range(2):
                        last = mm(ps_s[:, par, 0:PAIRS * WIN].rearrange("p (g k) -> p g k", g=PAIRS), neg_ident[:, :],
                                  smax[:, n % 2, par, :].unsqueeze(2).broadcast_to([128, PAIRS, WIN]),
                                  start=False, stop=True, skip_group_check=True)
                    last.then_inc(S["shift"], 1)

                def p_transpose(n):
                    ge("exp_done", n)
                    for g in range(PAIRS):
                        last = nc.tensor.transpose(ps_t[:, g // 3, (g % 3) * TOK:(g % 3 + 1) * TOK],
                                                   p_tok[:, n % 2, g].rearrange("p a k -> p (a k)"), ident[:, :])
                    last.then_inc(S["tp"], 1)

                def pv_product(n):
                    ge("ot_done", n - 1)
                    ge("v_lo", n)
                    ge("p_lo", n)
                    for g in range(PAIRS):
                        for i, (ps, vs) in enumerate(((0, 0), (0, 1), (1, 0))):
                            last = mm(ps_o[:, g * 4 * VW:(g + 1) * 4 * VW], pt[:, n % 2, ps, g, :],
                                      v_blk[:, n % 2, vs, g].rearrange("p a w d -> p (a w d)"),
                                      start=(i == 0), stop=(i == 2))
                    last.then_inc(S["pv"], 1)

                def o_transpose(n, held):
                    if held is not None:
                        ge("resid2", held)
                    ge("o_lo", n)
                    transpose3(ps_o16, os[:, n % 2]).then_inc(S["to"], 1)

                def projection(n):
                    layer, t = visit(n)
                    if live(n + 2):
                        ge("qk_lo", n + 2)
                    else:
                        ge("resid1", n - 1)
                    ge("ot_done", n)
                    contract(ps_qk[:, 0:C], w_proj[layer], lambda b: ot[:, n % 2, b, :], 0, C)\
                        .then_inc(S["pr"], 1)

                def norm2_transpose(n):
                    take_tr("ht_done", n)
                    ge("lo2", n)
                    transpose3(ps_tr16, xs[:, 1, n % 2]).then_inc(S["tr2"], 1)

                def hidden(m):
                    layer, _ = visit(p * GROUP)
                    u = p * HC + m
                    if m == 0:
                        ge("ht_done", p * GROUP + GROUP - 1)
                        ge("exp_done", min(s - 1, end))
                    if m >= 2:
                        ge("gelu", u - 2)
                    for i, (part, blk) in enumerate(((0, 0), (0, 2), (1, 0), (2, 1), (3, 1))):
                        last = mm(ps_s[:, u % 2, :], w_fc1[layer][:, part, m * 128:(m + 1) * 128],
                                  ht[:, p % 2, blk, :], start=(i == 0), stop=(i == 4))
                    last.then_inc(S["fc1"], 1)

                def mlp_out(n, bank):
                    layer, t = visit(n)
                    tok = slice((t % GROUP) * TOK, (t % GROUP + 1) * TOK)
                    if n % GROUP == 0:
                        ge("h_hi", p * HC + HC - 1)
                        ge("h_lo", p * HC + HC - 1)
                    for m in range(HC):
                        for i, (hs, ws) in enumerate(((0, 0), (0, 1), (1, 0))):
                            last = mm(bank[:, 0:C], hid16[:, hs, m, tok], w_fc2[layer][:, ws, m, :],
                                      start=(m == 0 and i == 0), stop=(m == HC - 1 and i == 2))
                    last.then_inc(S["fc2"], 1)

                def y_transpose(n):
                    layer, t = visit(n)
                    take_tr("y_ready", visit_in_layer(n))
                    ge("resid2", n)
                    for k in range(2):
                        last = nc.tensor.transpose(ps_tr[0:H2, k * TOK:(k + 1) * TOK], x_tok[:, t, k * H2:(k + 1) * H2],
                                                   ident[:, :])
                    last.then_inc(S["otr"], 1)

                p, place = mlp_phase(s)
                end = STEPS + GROUP - 1
                mlp = p >= -1
                in_o = p * GROUP + (0, 0, 2, 3)[place] if mlp and place else None
                last_block = mlp and visit(p * GROUP)[0] == 1
                if live(s):
                    qk_product(s)
                if live(s - 1):
                    p_transpose(s - 1)
                if mlp and place == 0:
                    hidden(0)
                if live(s):
                    v_product(s)
                if mlp and place == 0:
                    hidden(1)
                elif mlp:
                    if last_block and place == 2:
                        y_transpose(p * GROUP + 1)
                    ge("o_evac", min(s - 2, end))
                    if s - 2 > end:
                        ge("resid2", in_o - 1)
                        ge("ot_done", end)
                    mlp_out(in_o, ps_o)
                if live(s + 1) and not (mlp and place == 0):
                    norm1_transpose(s + 1)
                if live(s):
                    qk_transpose(s)
                if mlp and place == 0:
                    hidden(2)
                    hidden(3)
                if live(s - 2):
                    o_transpose(s - 2, in_o)
                if mlp and place == 0:
                    if live(s + 1):
                        norm1_transpose(s + 1)
                    hidden(4)
                    if live(s + 4) and visit(s + 4)[0] == 0:
                        x_transpose(s + 4)
                    hidden(5)
                    if live(s - 1):
                        pv_product(s - 1)
                elif mlp and place == 1:
                    ge("v_lo", min(s, end))
                    mlp_out(p * GROUP + 1, ps_v)
                if live(s):
                    scores(s)
                if not (mlp and place == 0):
                    if live(s + 4) and visit(s + 4)[0] == 0:
                        x_transpose(s + 4)
                    if live(s - 1):
                        pv_product(s - 1)
                    if last_block:
                        y_transpose(p * GROUP + place - (place == 1))
                if live(s - 2):
                    projection(s - 2)
                if live(s - 3) and mlp and place == 0:
                    norm2_transpose(s - 3)
                if live(s):
                    shift_scores(s)
                if live(s - 3) and not (mlp and place == 0):
                    norm2_transpose(s - 3)

            tr_reader = ["x_in", -1]
            run(pe, slot)

        @block.scalar
        def _(act):
            copy = nc.scalar.activation
            for name in ("x_in", "xt_done", "hi1", "qk_hi", "v_hi", "k_evac", "exp_done", "p_hi", "o_evac", "o_hi",
                         "hi2", "ht_done", "gelu", "y_ready"):
                act.sem_inc(S[name], CREDIT)
            act.wait_ge(made, 1 + 4 * LAYERS)

            def slot(it, s, live):
                def ge(name, n):
                    when(act, it, name, n)

                def x_evac(n):
                    ge("xtr", visit_in_layer(n))
                    copy(stream(n, 0), ps_tr[:, 0:C], ACT.Copy).then_inc(S["x_in"], 1)

                def norm_hi(n, which):
                    a = "12"[which]
                    ge("ln" + a, n)
                    ge("tr" + a, n - 2)
                    copy(xs[:, which, n % 2, 0, :], xn[:, which, n % 2, :], ACT.Copy).then_inc(S["hi" + a], 1)

                def xt_evac(n):
                    ge("tr1", n)
                    copy(xt[:, n % 2].rearrange("p b t -> p (b t)"), ps_tr16[:, 0:3 * TOK], ACT.Copy)\
                        .then_inc(S["xt_done"], 1)

                def ht_evac(n):
                    ge("tr2", n)
                    copy(ht[:, n // GROUP % 2, :, (n % GROUP) * TOK:(n % GROUP + 1) * TOK],
                         ps_tr16[:, 0:3 * TOK].rearrange("p (b t) -> p b t", b=3), ACT.Copy).then_inc(S["ht_done"], 1)

                def qk_hi(n):
                    ge("qk_mm", n)
                    for i, places in enumerate((slice(0, 2), slice(0, 3, 2))):
                        src = ps_qk[:, i * C:(i + 1) * C].rearrange("p (h d) -> p h d", d=HD).unsqueeze(2)
                        last = copy(qk[:, n % 2, i * HEADS:(i + 1) * HEADS, places, :],
                                    src.broadcast_to([128, HEADS, 2, HD]), ACT.Copy, scale=UNSCALE)
                    last.then_inc(S["qk_hi"], 1)

                def v_hi(n):
                    ge("v_mm", n)
                    for par in range(2):
                        for w in range(2):
                            src, dst = v_places(n, par, w, 0)
                            last = copy(dst, src, ACT.Copy, scale=UNSCALE)
                    last.then_inc(S["v_hi"], 1)

                def k_evac(n):
                    ge("tqk", n)
                    copy(kt[:, n % 2].rearrange("p g t -> p (g t)"), ps_t16[1][:, 0:PAIRS * TOK], ACT.Copy)\
                        .then_inc(S["k_evac"], 1)

                def exp(n):
                    ge("shift", n)
                    nc.scalar.activation(p_tok[:, n % 2].rearrange("p g a k -> p a g k"),
                                         ps_s[:, :, 0:PAIRS * WIN].rearrange("p a (g k) -> p a g k", g=PAIRS),
                                         ACT.Exp).then_inc(S["exp_done"], 1)

                def p_hi(n):
                    ge("tp", n)
                    copy(pt[:, n % 2, 0].rearrange("p (b g) t -> p b (g t)", b=2), ps_t[:, :, 0:3 * TOK], ACT.Copy)\
                        .then_inc(S["p_hi"], 1)

                def o_evac(n):
                    ge("pv", n)
                    for w in range(2):
                        rows = slice(w * WIN, (w + 1) * WIN)
                        src = ps_o[rows, 0:4 * PAIRS * VW].rearrange("p (h w d) -> p h w d", w=2, d=VW)[:, :, w]
                        last = copy(o_raw[rows, n % 2], src, ACT.Copy)
                    last.then_inc(S["o_evac"], 1)

                def o_hi(n):
                    ge("o_norm", n)
                    copy(os[:, n % 2, 0, :], o_tok[:, n % 2, :], ACT.Copy).then_inc(S["o_hi"], 1)

                def gelu(m):
                    layer, _ = visit(p * GROUP)
                    u = p * HC + m
                    ge("fc1", u)
                    ge("h_hi", u - 2)
                    ge("h_lo", u - 2)
                    nc.scalar.activation(hid[:, u % 2, :], ps_s[:, u % 2, :], ACT.Gelu, bias=b_fc1[layer][:, m:m + 1],
                                         scale=UNSCALE).then_inc(S["gelu"], 1)

                def y_evac(n):
                    layer, t = visit(n)
                    ge("otr", visit_in_layer(n))
                    if t == 0:
                        act.wait_ge(y_stored, it * 16 + 16)
                    tile = ps_tr[0:H2, 0:2 * TOK].rearrange("p (k t) -> p k t", k=2)
                    for win, img in box_pairs(t, tile, y_img[:, :, :]):
                        last = copy(img, win, ACT.Copy)
                    last.then_inc(S["y_ready"], 1)

                p, place = mlp_phase(s)
                mlp = p >= -1
                hid_slot = mlp and place == 0
                last_block = mlp and visit(p * GROUP)[0] == 1
                if live(s):
                    qk_hi(s)
                if live(s - 1):
                    p_hi(s - 1)
                if hid_slot:
                    gelu(0)
                if live(s):
                    v_hi(s)
                if hid_slot:
                    gelu(1)
                if live(s - 3):
                    norm_hi(s - 3, 1)
                if last_block and place == 2:
                    y_evac(p * GROUP + 1)
                if live(s + 1) and not hid_slot:
                    xt_evac(s + 1)
                if live(s):
                    k_evac(s)
                if hid_slot:
                    gelu(2)
                    gelu(3)
                    if live(s + 1):
                        xt_evac(s + 1)
                    gelu(4)
                if live(s + 4) and visit(s + 4)[0] == 0:
                    x_evac(s + 4)
                if hid_slot:
                    gelu(5)
                if live(s + 2):
                    norm_hi(s + 2, 0)
                if live(s - 1):
                    o_evac(s - 1)
                if last_block and not hid_slot:
                    y_evac(p * GROUP + place - (place == 1))
                if live(s - 3) and hid_slot:
                    ht_evac(s - 3)
                if live(s):
                    exp(s)
                if live(s - 1):
                    o_hi(s - 1)
                if live(s - 3) and not hid_slot:
                    ht_evac(s - 3)

            run(act, slot)

        @block.vector
        def _(dve):
            v = nc.vector
            for name in ("bn1a", "bn1", "lo1", "qk_lo", "v_lo", "q_evac", "max_done", "p_lo", "inv_done", "o_lo",
                         "ot_done", "resid1", "bn2a", "bn2", "lo2", "h_lo", "resid2"):
                dve.sem_inc(S[name], CREDIT)

            steps = [0]

            def link(ins):
                steps[0] += 1
                ins.then_inc(dve_chain, 1)
                dve.wait_ge(dve_chain, steps[0])

            v.memset(ones16[:, :], 1.0)
            v.memset(ones_row[:, :], 1.0)
            v.memset(half[:, :], -0.5)
            v.memset(x_tok[:, :, :].rearrange("p t c -> p (t c)"), 0.0)
            for l in range(LAYERS):
                v.memset(b_qk[l][:, :], 0.0)
            v.memset(qk[:, :].rearrange("p r h s d -> p (r h s d)"), 0.0)
            link(v.memset(v_blk[:, :].rearrange("p r s g a w d -> p (r s g a w d)"), 0.0))
            for par in range(2):
                for r in range(2):
                    v.memset(v_blk[par * 64:par * 64 + 64, r, 0, :, par, :, HD:VW], 1.0)
            dve.wait_ge(const_in[0], 16)
            link(v.tensor_copy(ident16[:, :], ident[:, :]))
            v.tensor_scalar(neg_ident[:, :], ident[:, :], -1.0, None, ALU.mult).then_inc(made, 1)

            def split(hi, lo, src):
                link(v.tensor_copy(hi, src))
                link(v.tensor_tensor(lo, src, hi, ALU.subtract))

            def make_weight(w, n, gain, q_cols=0):
                for ab in range(2):
                    for c0, c1, s in ((0, q_cols, WSCALE * QSCALE), (q_cols, n, WSCALE)):
                        if c1 > c0:
                            src, dst = stage[:, ab, c0:c1], scaled[:, ab, c0:c1]
                            if gain is None:
                                link(v.tensor_scalar(dst, src, s, None, ALU.mult))
                            else:
                                link(v.tensor_scalar(dst, src, gain[:, ab:ab + 1], s, ALU.mult, ALU.mult))
                    split(w[:, 2 * ab, 0:n], w[:, 2 * ab + 1, 0:n], scaled[:, ab, 0:n])

            for l in range(LAYERS):
                dve.wait_ge(norm_in[l], 16 * 12)
                dve.wait_ge(w_in[4 * l], 16 * W_DMAS[0])
                make_weight(w_qkv[l], 3 * C, cols[:, l, 0, :], q_cols=C)
                dve.wait_ge(folded, 4 * l + 1)
                link(v.tensor_tensor(row[:, 0:2 * C], row[:, 0:2 * C], ps_qk[0:1, 0:2 * C], ALU.add))
                link(v.tensor_scalar(row[:, 0:C], row[:, 0:C], WSCALE * QSCALE, None, ALU.mult))
                link(v.tensor_scalar(row[:, C:2 * C], row[:, C:2 * C], WSCALE, None, ALU.mult))
                split(b_qk[l][0:1, :], b_qk[l][32:33, :], row[:, 0:2 * C])
                link(v.tensor_tensor(vcol[:, 0:1], vcol[:, 0:1], ps_v[:, 0:1], ALU.add))
                v.tensor_tensor(vcol[0:CB, 1:2], vcol[0:CB, 1:2], ps_v[0:CB, 1:2], ALU.add).then_inc(made, 1)
                dve.wait_ge(w_in[4 * l + 1], 16 * W_DMAS[1])
                make_weight(w_proj[l], C, None)
                dve.wait_ge(folded, 4 * l + 2)
                link(v.tensor_tensor(rowsum[:, 0:C], row[:, 3 * C:4 * C], ps_o[0:1, 0:C], ALU.add))
                v.tensor_copy(rowsum[:, C:2 * C], row[:, 4 * C:5 * C]).then_inc(made, 1)
                dve.wait_ge(w_in[4 * l + 2], 16 * W_DMAS[2])
                make_weight(w_fc1[l], HID, cols[:, l, 2, :])
                dve.wait_ge(folded, 4 * l + 3)
                v.tensor_tensor(b_fc1[l][:, :], b_fc1[l][:, :], ps_s[:, 0, 0:HC], ALU.add).then_inc(made, 1)
                dve.wait_ge(w_in[4 * l + 3], 16 * W_DMAS[3])
                flat = stage[:, :, :].rearrange("p a n -> p (a n)")[:, 0:HC * C]
                flat2 = scaled[:, :, :].rearrange("p a n -> p (a n)")[:, 0:HC * C]
                link(v.tensor_scalar(flat2, flat, WSCALE, None, ALU.mult))
                split(w_fc2[l][:, 0].rearrange("p m c -> p (m c)"), w_fc2[l][:, 1].rearrange("p m c -> p (m c)"), flat2)
                dve.wait_ge(folded, 4 * l + 4)
                link(v.tensor_copy(b_proj[l][:, :], ps_t[:, 0, 0:C]))
                v.tensor_copy(b_fc2[l][:, :], ps_t[:, 0, C:2 * C]).then_inc(made, 1)
            dve.wait_ge(const_in[2], 16 * 2 * WS)
            for key in range(WIN):
                last = v.tensor_copy(rel_t[:, :, :, key], rel[:, WIN - 1 - key, :].rearrange("p (g a) -> p a g", a=2))
            link(last)
            dve.wait_ge(const_in[1], 16)
            for kind in range(4):
                for par in range(2):
                    link(v.tensor_tensor(rel_m[:, par], rel_t[:, par],
                                         mask[:, kind, :].unsqueeze(1).broadcast_to([128, PAIRS, WIN]), ALU.add))
                link(v.tensor_copy(bias_tab[:, kind, 0], rel_m[:, :]))
                last = v.tensor_tensor(bias_tab[:, kind, 1], rel_m[:, :], bias_tab[:, kind, 0], ALU.subtract)
                if kind < 3:
                    link(last)
            last.then_inc(tables, 1)

            def slot(it, s, live):
                def ge(name, n):
                    when(dve, it, name, n)

                def statistics(n, which):
                    a = "12"[which]
                    layer, _ = visit(n)
                    if which == 1:
                        ge("resid1", n)
                    elif layer == 0:
                        ge("x_in", visit_in_layer(n))
                    elif n >= STEPS - GROUP or s >= FIRST:
                        ge("resid2", n - 3 * GROUP)
                    v.bn_stats(bn6[:, which, n % 2, :], stream(n, which)).then_inc(S[f"bn{a}a"], 1)

                def mean_variance(n, which):
                    a = "12"[which]
                    ge(f"bn{a}a", n)
                    ge("ln" + a, n - 2)
                    dve.nop(nofuse=True)
                    v.bn_aggr(mv[:, which, n % 2, :], bn6[:, which, n % 2, :]).then_inc(S["bn" + a], 1)

                def norm_lo(n, which):
                    a = "12"[which]
                    ge("hi" + a, n)
                    v.tensor_tensor(xs[:, which, n % 2, 1, :], xn[:, which, n % 2, :], xs[:, which, n % 2, 0, :],
                                    ALU.subtract).then_inc(S["lo" + a], 1)

                def qk_lo(n):
                    ge("qk_hi", n)
                    for i, place in enumerate((2, 1)):
                        heads = slice(i * HEADS, (i + 1) * HEADS)
                        last = v.scalar_tensor_tensor(
                            out=qk[:, n % 2, heads, place, :],
                            in0=ps_qk[:, i * C:(i + 1) * C].rearrange("p (h d) -> p h d", d=HD), scalar=UNSCALE,
                            in1=qk[:, n % 2, heads, 0, :], op0=ALU.mult, op1=ALU.subtract)
                    last.then_inc(S["qk_lo"], 1)

                def v_lo(n):
                    ge("v_hi", n)
                    for par in range(2):
                        for w in range(2):
                            src, dst = v_places(n, par, w, 1)
                            last = v.scalar_tensor_tensor(out=dst, in0=src, scalar=UNSCALE,
                                                          in1=v_places(n, par, w, 0)[1],
                                                          op0=ALU.mult, op1=ALU.subtract)
                    last.then_inc(S["v_lo"], 1)

                def q_evac(n):
                    ge("tqk", n)
                    v.tensor_copy(qt[:, n % 2].rearrange("p g t -> p (g t)"), ps_t16[0][:, 0:PAIRS * TOK])\
                        .then_inc(S["q_evac"], 1)

                def row_max(n):
                    ge("s_mm", n)
                    v.tensor_reduce(smax[:, n % 2], ps_s[:, :, 0:PAIRS * WIN].rearrange("p a (g k) -> p a g k", g=PAIRS),
                                    AX.X, ALU.max).then_inc(S["max_done"], 1)

                def p_lo(n):
                    ge("p_hi", n)
                    v.tensor_tensor(pt[:, n % 2, 1].rearrange("p (b g) t -> p b (g t)", b=2), ps_t[:, :, 0:3 * TOK],
                                    pt[:, n % 2, 0].rearrange("p (b g) t -> p b (g t)", b=2), ALU.subtract)\
                        .then_inc(S["p_lo"], 1)

                def inverse_sums(n):
                    ge("o_evac", n)
                    v.reciprocal(o_inv[:, n % 2, :], o_raw[:, n % 2, :, HD]).then_inc(S["inv_done"], 1)

                def o_lo(n):
                    ge("o_hi", n)
                    v.tensor_tensor(os[:, n % 2, 1, :], o_tok[:, n % 2, :], os[:, n % 2, 0, :], ALU.subtract)\
                        .then_inc(S["o_lo"], 1)

                def ot_evac(n):
                    ge("to", n)
                    v.tensor_copy(ot[:, n % 2].rearrange("p b t -> p (b t)"), ps_o16[:, 0:3 * TOK])\
                        .then_inc(S["ot_done"], 1)

                def residual(n, src, out, old, product, bias, done):
                    ge(product, n)
                    ge(bias, n)
                    v.scalar_tensor_tensor(out=out, in0=src, scalar=UNSCALE, in1=old,
                                           op0=ALU.mult, op1=ALU.add).then_inc(S[done], 1)

                def attention_residual(n):
                    residual(n, ps_qk[:, 0:C], stream(n, 1), stream(n, 0), "pr", "bias1", "resid1")

                def mlp_residual(n, bank):
                    residual(n, bank[:, 0:C], x_tok[:, visit(n)[1], :], stream(n, 1), "fc2", "bias2", "resid2")

                def hidden_lo(m):
                    u = p * HC + m
                    ge("gelu", u)
                    ge("h_hi", u)
                    v.tensor_tensor(hid16[:, 1, m, :], hid[:, u % 2, :], hid16[:, 0, m, :], ALU.subtract)\
                        .then_inc(S["h_lo"], 1)

                p, place = mlp_phase(s)
                mlp = p >= -1
                hid_slot = mlp and place == 0
                if live(s):
                    qk_lo(s)
                if live(s - 1):
                    p_lo(s - 1)
                if live(s):
                    v_lo(s)
                if hid_slot:
                    hidden_lo(0)
                elif mlp:
                    mlp_residual(p * GROUP + (0, 0, 2, 3)[place], ps_o)
                if live(s):
                    q_evac(s)
                if hid_slot:
                    hidden_lo(1)
                if live(s - 2):
                    ot_evac(s - 2)
                if hid_slot:
                    hidden_lo(2)
                    hidden_lo(3)
                if live(s - 3):
                    norm_lo(s - 3, 1)
                if hid_slot:
                    hidden_lo(4)
                if mlp and place == 1:
                    mlp_residual(p * GROUP + 1, ps_v)
                if live(s):
                    row_max(s)
                if hid_slot:
                    hidden_lo(5)
                if live(s - 1):
                    inverse_sums(s - 1)
                if live(s - 2):
                    attention_residual(s - 2)
                    statistics(s - 2, 1)
                if live(s + 2):
                    norm_lo(s + 2, 0)
                if live(s - 2):
                    mean_variance(s - 2, 1)
                if live(s + 4):
                    statistics(s + 4, 0)
                if live(s - 1):
                    o_lo(s - 1)
                if live(s + 4):
                    mean_variance(s + 4, 0)

            run(dve, slot)

        @block.gpsimd
        def _(pool):
            g_ = nc.gpsimd
            for name in ("ln1a", "ln1b", "ln1", "bias1", "o_norm", "ln2a", "ln2b", "ln2", "bias2", "h_hi"):
                pool.sem_inc(S[name], CREDIT)

            def order_tile(t):
                for win, img in box_pairs(t, x_win[:, :, t * TOK:(t + 1) * TOK], x_img[:, :, :]):
                    last = g_.tensor_scalar(win, img, 1.0, 0.0, ALU.mult, ALU.add)
                if t == TILES - 1:
                    last.then_inc(x_ordered, 1)

            pool.wait_ge(x_loaded, 16)
            for t in range(TILES):
                order_tile(t)
            pool.wait_ge(made, 1 + 4 * LAYERS)

            def slot(it, s, live):
                def ge(name, n):
                    when(pool, it, name, n)

                def normalize(n, which):
                    a, r = "12"[which], n % 2
                    ge("bn" + a, n)
                    ge("lo" + a, n - 2)
                    pool.nop(nofuse=True)
                    g_.tensor_scalar(nmean[:, which, r:r + 1], mv[:, which, r, 0:1], -1.0, 0.0, ALU.mult, ALU.add)
                    g_.tensor_scalar(vare[:, which, r:r + 1], mv[:, which, r, 1:2], EPS, 1.0, ALU.add, ALU.mult)\
                        .then_inc(S[f"ln{a}a"], 1)
                    ge(f"ln{a}a", n)
                    g_.tensor_tensor(rstd[:, which, r:r + 1], vare[:, which, r:r + 1], half[:, :], ALU.pow)\
                        .then_inc(S[f"ln{a}b"], 1)
                    ge(f"ln{a}b", n)
                    pool.nop(nofuse=True)
                    g_.tensor_scalar(xn[:, which, r, :], stream(n, which), nmean[:, which, r:r + 1],
                                     rstd[:, which, r:r + 1], ALU.add, ALU.mult).then_inc(S["ln" + a], 1)
                    bias = (b_proj, b_fc2)[which][visit(n)[0]]
                    g_.tensor_tensor(stream(n, which), stream(n, which), bias[:, :], ALU.add).then_inc(S["bias" + a], 1)

                def o_norm(n):
                    ge("inv_done", n)
                    g_.tensor_tensor(o_tok[:, n % 2, :].rearrange("p (h d) -> p h d", d=HD), o_raw[:, n % 2, :, 0:HD],
                                     o_inv[:, n % 2, :].unsqueeze(2).broadcast_to([128, HEADS, HD]), ALU.mult)\
                        .then_inc(S["o_norm"], 1)

                def hidden_hi(m):
                    u = p * HC + m
                    ge("gelu", u)
                    pool.nop(nofuse=True)
                    g_.tensor_scalar(hid16[:, 0, m, :], hid[:, u % 2, :], 1.0, 0.0, ALU.mult, ALU.add)\
                        .then_inc(S["h_hi"], 1)

                p, place = mlp_phase(s)
                hid_slot = p >= -1 and place == 0
                if live(s - 3):
                    normalize(s - 3, 1)
                if live(s + 3):
                    normalize(s + 3, 0)
                if hid_slot:
                    for m in range(HC):
                        hidden_hi(m)
                if live(s - 1):
                    o_norm(s - 1)
                if GROUP <= s < 2 * GROUP:
                    if s == GROUP:
                        ge("xtr", TILES - 1)
                        pool.wait_ge(x_loaded, it * 16 + 32)
                        pool.nop(nofuse=True)
                    for t in range(2 * (s - GROUP), 2 * (s - GROUP) + 2):
                        order_tile(t)

            run(pool, slot)


_BLOCKS = [
    {"wqkv": "L0_conv_qkv_w", "bqkv": "L0_conv_qkv_b", "wproj": "L0_conv_proj_w", "bproj": "L0_conv_proj_b",
     "g1": "L0_conv_norm1_g", "b1": "L0_conv_norm1_b", "g2": "L0_conv_norm2_g", "b2": "L0_conv_norm2_b",
     "wfc1": "L0_conv_fc1_w", "bfc1": "L0_conv_fc1_b", "wfc2": "L0_conv_fc2_w", "bfc2": "L0_conv_fc2_b"},
    {"wqkv": "L1_conv_w_qkv", "bqkv": "L1_conv_b_qkv", "wproj": "L1_conv_w_proj", "bproj": "L1_conv_b_proj",
     "g1": "L1_conv_gamma1", "b1": "L1_conv_beta1", "g2": "L1_conv_gamma2", "b2": "L1_conv_beta2",
     "wfc1": "L1_conv_w_fc1", "bfc1": "L1_conv_b_fc1", "wfc2": "L1_conv_w_fc2", "bfc2": "L1_conv_b_fc2"},
]


def _constants(np):
    ident = np.eye(128, dtype=np.float32)
    mask = np.zeros((128, 4, WIN), np.float32)
    r, c = np.divmod(np.arange(WIN), WS)
    for kind in range(4):
        for w in range(2):
            apart = np.zeros((WIN, WIN), bool)
            if kind // 2:
                apart |= (r[:, None] < SHIFT) != (r[None] < SHIFT)
            if kind % 2 and w == 1:
                apart |= (c[:, None] < SHIFT) != (c[None] < SHIFT)
            mask[w * WIN:(w + 1) * WIN, kind] = np.where(apart, np.float32(-10.0), np.float32(0.0))
    return ident, mask


def kernel(**inputs):
    import numpy as _np
    import concourse.bacc as _bacc
    from concourse import mybir as _mybir
    from concourse.bass_utils import run_bass_kernel_spmd as _run

    nc = _bacc.Bacc("TRN2", target_bir_lowering=False, num_devices=1)
    ident, mask = _constants(_np)
    given = {k: inputs[k] for k in inputs} | {"const_ident": ident, "const_mask": mask}
    arrays, args = {}, {}
    for name, a in given.items():
        a = _np.ascontiguousarray(a)
        arrays[f"in_{name}_dram"] = a
        args[name] = nc.dram_tensor(f"in_{name}_dram", a.shape, _mybir.dt.from_np(a.dtype), kind="ExternalInput").ap()
    out = nc.dram_tensor("out_0_dram", (IMAGES, C, SIDE, SIDE), _mybir.dt.float32, kind="ExternalOutput").ap()
    layers = [{k: args[v] for k, v in b.items()} for b in _BLOCKS]
    swin_program(nc, args["x"], layers, args["L0_conv_rel_bias"], args["const_ident"], args["const_mask"], out)
    r = _run(nc, [arrays], core_ids=[0])
    return r.results[0]["out_0_dram"]
```

```python
from contextlib import ExitStack

import concourse.bass as bass
from concourse import mybir

F32 = mybir.dt.float32
F16 = mybir.dt.float16
BF16 = mybir.dt.bfloat16
ALU = mybir.AluOpType
ACT = mybir.ActivationFunctionType
AX = mybir.AxisListType

IMAGES, C, SIDE = 32, 192, 32
HEADS, HD = 12, 16
PAIRS = HEADS // 2
WS, SHIFT = 8, 4
WIN = WS * WS
TOK = 2 * WIN
TILES = SIDE * SIDE // TOK
LAYERS = 2
STEPS = LAYERS * TILES
GROUP = 4
PHASES = STEPS // GROUP
HID = 4 * C
HC = HID // 128
CB = 64
WSCALE = 64.0
UNSCALE = 1.0 / WSCALE
QSCALE = HD ** -0.5
VW = HD + 1
CREDIT = 4
FIRST, LAST = 4, 4 + STEPS
EPS = 1e-5


def visit(n):
    layer, group = ((1, 1), (0, 1), (1, 0), (0, 0))[n // GROUP % PHASES]
    return layer, group * GROUP + n % GROUP


def visit_in_layer(n):
    layer, _ = visit(n)
    return (n + (0 if layer else GROUP)) // (2 * GROUP) * GROUP + n % GROUP


def mlp_phase(s):
    return (s - FIRST) // GROUP - 1, (s - FIRST) % GROUP


def window_pieces(t):
    i, jp = t // 2, t % 2
    rows = [(0, WS, WS * i + SHIFT)] if i < 3 else [(0, SHIFT, SIDE - SHIFT), (SHIFT, SHIFT, 0)]
    cols = [(0, 2, 0, WS, SHIFT)] if jp == 0 else [
        (0, 1, 0, WS, 2 * WS + SHIFT), (1, 1, 0, SHIFT, SIDE - SHIFT), (1, 1, SHIFT, SHIFT, 0)]
    return [(w0, nw, r0, nr, c0, nc, row, col) for r0, nr, row in rows for w0, nw, c0, nc, col in cols]


def box_pairs(t, tile_view, image_view):
    tv = tile_view.rearrange("p k (w r c) -> p k w r c", w=2, r=WS)
    iv = image_view.rearrange("p k (r c) -> p k r c", r=SIDE)
    out = []
    for w0, nw, r0, nr, c0, nc, row, col in window_pieces(t):
        if nw == 2:
            for k in range(2):
                out.append((tv[:, k, :, r0:r0 + nr, :],
                            iv[:, k, row:row + nr, col:col + 2 * WS].rearrange("p r (w c) -> p w r c", w=2)))
        else:
            out.append((tv[:, :, w0, r0:r0 + nr, c0:c0 + nc], iv[:, :, row:row + nr, col:col + nc]))
    return out


def swin_program(nc, x, layers, rel_bias, ident_in, mask_in, out):
    H2 = C // 2
    with ExitStack() as ctx:
        def sb(name, shape, dt):
            return ctx.enter_context(nc.sbuf_tensor(name, shape, dt))

        def sem(name):
            return ctx.enter_context(nc.semaphore(name))

        banks = [ctx.enter_context(nc.psum_tensor(f"bank{i}", [128, 512], F32)) for i in range(4)]
        ps_s = ctx.enter_context(nc.psum_tensor("ps_s", [128, 2, 512], F32))
        ps_t = ctx.enter_context(nc.psum_tensor("ps_t", [128, 2, 512], F32))
        ps_tr, ps_o, ps_qk, ps_v = banks
        ps_tr16 = ps_tr[:, :].bitcast(F16)
        ps_o16 = ps_o[:, :].bitcast(F16)
        ps_t16 = [ps_t[:, i, :].bitcast(F16) for i in range(2)]

        ident = sb("ident", [128, 128], F32)
        ident16 = sb("ident16", [128, 128], F16)
        neg_ident = sb("neg_ident", [128, 128], BF16)
        ones16 = sb("ones16", [128, 128], F16)
        ones_row = sb("ones_row", [1, 128], F32)
        mask = sb("mask", [128, 4, WIN], F32)
        rel = sb("rel", [128, WIN, HEADS], F32)
        rel_t = sb("rel_t", [128, 2, PAIRS, WIN], F32)
        rel_m = sb("rel_m", [128, 2, PAIRS, WIN], F32)
        bias_tab = sb("bias_tab", [128, 4, 2, 2, PAIRS, WIN], F16)
        stage = sb("stage", [128, 2, HID], F32)
        scaled = sb("scaled", [128, 2, HID], F32)
        cols = sb("cols", [128, LAYERS, 4, 2], F32)
        vcol = sb("vcol", [128, 2], F32)
        row = sb("row", [1, 5 * C], F32)
        rowsum = sb("rowsum", [1, 2 * C], F32)
        w_qkv = [sb(f"w_qkv{l}", [128, 4, 3 * C], F16) for l in range(LAYERS)]
        w_proj = [sb(f"w_proj{l}", [128, 4, C], F16) for l in range(LAYERS)]
        w_fc1 = [sb(f"w_fc1{l}", [128, 4, HID], F16) for l in range(LAYERS)]
        w_fc2 = [sb(f"w_fc2{l}", [128, 2, HC, C], F16) for l in range(LAYERS)]
        b_qk = [sb(f"b_qk{l}", [128, 2 * C], F16) for l in range(LAYERS)]
        b_proj = [sb(f"b_proj{l}", [128, C], F32) for l in range(LAYERS)]
        b_fc1 = [sb(f"b_fc1{l}", [128, HC], F32) for l in range(LAYERS)]
        b_fc2 = [sb(f"b_fc2{l}", [128, C], F32) for l in range(LAYERS)]

        x_img = sb("x_img", [H2, 2, SIDE * SIDE], F32)
        x_win = sb("x_win", [H2, 2, SIDE * SIDE], F32)
        y_img = sb("y_img", [H2, 2, SIDE * SIDE], F32)
        x_new = sb("x_new", [128, GROUP, C], F32)
        x_mid = sb("x_mid", [128, GROUP, C], F32)
        x_tok = sb("x_tok", [128, TILES, C], F32)
        bn6 = sb("bn6", [128, 2, 2, 6], F32)
        mv = sb("mv", [128, 2, 2, 2], F32)
        nmean = sb("nmean", [128, 2, 2], F32)
        vare = sb("vare", [128, 2, 2], F32)
        rstd = sb("rstd", [128, 2, 2], F32)
        half = sb("half", [128, 1], F32)
        spare = sb("spare", [1, 1], F32)
        xn = sb("xn", [128, 2, 2, C], F32)
        xs = sb("xs", [128, 2, 2, 2, C], F16)
        xt = sb("xt", [128, 2, 3, TOK], F16)
        ht = sb("ht", [128, 2, 3, GROUP * TOK], F16)
        qk = sb("qk", [128, 2, 2 * HEADS, 4, HD], F16)
        qt = sb("qt", [128, 2, PAIRS, TOK], F16)
        kt = sb("kt", [128, 2, PAIRS, TOK], F16)
        v_blk = sb("v_blk", [128, 2, 2, PAIRS, 2, 2, VW], F16)
        smax = sb("smax", [128, 2, 2, PAIRS], BF16)
        p_tok = sb("p_tok", [128, 2, PAIRS, 2, WIN], F32)
        pt = sb("pt", [128, 2, 2, PAIRS, TOK], F16)
        o_raw = sb("o_raw", [128, 2, HEADS, VW], F32)
        o_inv = sb("o_inv", [128, 2, HEADS], F32)
        o_tok = sb("o_tok", [128, 2, C], F32)
        os = sb("os", [128, 2, 2, C], F16)
        ot = sb("ot", [128, 2, 3, TOK], F16)
        hid = sb("hid", [128, 2, GROUP * TOK], F32)
        hid16 = sb("hid16", [128, 2, HC, GROUP * TOK], F16)

        const_in = [sem(f"const_in{i}") for i in range(3)]
        norm_in = [sem(f"norm_in{l}") for l in range(LAYERS)]
        w_in = [sem(f"w_in{j}") for j in range(4 * LAYERS)]
        folded = sem("folded")
        made = sem("made")
        dve_chain = sem("dve_chain")
        tables = sem("tables")

        COUNT = {name: STEPS for name in (
            "bn1a bn1 ln1a ln1b ln1 bias1 hi1 lo1 tr1 xt_done qk_mm v_mm qk_hi qk_lo v_hi v_lo tqk q_evac "
            "k_evac s_mm max_done shift exp_done tp p_hi p_lo pv o_evac inv_done o_norm o_hi o_lo to ot_done "
            "pr resid1 bn2a bn2 ln2a ln2b ln2 bias2 hi2 lo2 tr2 ht_done fc2 resid2").split()}
        AHEAD = dict.fromkeys(COUNT, GROUP)
        COUNT |= {name: PHASES * HC for name in ("fc1", "gelu", "h_hi", "h_lo")}
        AHEAD |= {name: HC for name in ("fc1", "gelu", "h_hi", "h_lo")}
        COUNT |= {name: TILES for name in ("xtr", "x_in", "otr", "y_ready")}
        AHEAD |= {name: 0 for name in ("xtr", "x_in", "otr", "y_ready")}
        COUNT["exp_loaded"], AHEAD["exp_loaded"] = PHASES, 1
        S = {name: sem(name) for name in COUNT}
        x_loaded = sem("x_loaded")
        x_ordered = sem("x_ordered")
        y_stored = sem("y_stored")

        def when(eng, it, name, n):
            eng.wait_ge(S[name], it * COUNT[name] + (n + 1 + AHEAD[name] + CREDIT))

        def stream(n, which):
            layer, t = visit(n)
            return x_tok[:, t, :] if layer else (x_new, x_mid)[which][:, t % GROUP, :]

        def run(eng, slot):
            for s in range(-2 * GROUP, FIRST):
                slot(0, s, lambda n: n >= -GROUP)
            with eng.Fori(0, IMAGES) as it:
                for s in range(FIRST, LAST):
                    slot(it, s, lambda n: True)
            for s in range(LAST, STEPS + GROUP + 8):
                slot(IMAGES - 1, s, lambda n: n < STEPS + GROUP)

        def v_places(n, par, w, part):
            src = ps_v[w * WIN:(w + 1) * WIN, 0:C].rearrange("p (g a d) -> p g a d", a=2, d=HD)[:, :, par]
            return src, v_blk[par * 64:par * 64 + 64, n % 2, part, :, par, w, 0:HD]

        block = ctx.enter_context(nc.Block())
        A, B = slice(CB, C), slice(0, CB)

        @block.sync
        def _(sp):
            sp.sem_inc(y_stored, 16)
            sp.dma_start(x_img[:, :, :], x[0].rearrange("(k p) h w -> p k (h w)", k=2)).then_inc(x_loaded, 16)
            sp.dma_start(ident[:, :], ident_in).then_inc(const_in[0], 16)
            sp.dma_start(mask[:, :, :], mask_in).then_inc(const_in[1], 16)
            span = 2 * WS - 1
            for w in range(2):
                for qr in range(WS):
                    src = bass.AP(tensor=rel_bias.tensor, offset=rel_bias.offset + qr * span * HEADS,
                                  ap=[[HEADS, WS], [span * HEADS, WS], [HEADS, WS], [1, HEADS]])
                    p0 = w * WIN + qr * WS
                    sp.dma_start(rel[p0:p0 + WS, :, :].rearrange("p (a b) h -> p a b h", a=WS), src)\
                        .then_inc(const_in[2], 16)
            for l, L in enumerate(layers):
                for i, name in enumerate(("g1", "b1", "g2", "b2")):
                    v = L[name].rearrange("(c a) -> c a", a=1)
                    sp.dma_start(cols[:, l, i, 0:1], v[A, :]).then_inc(norm_in[l], 16)
                    sp.dma_start(cols[0:CB, l, i, 1:2], v[B, :]).then_inc(norm_in[l], 16)
                    sp.dma_start(cols[CB:128, l, i, 1:2], v[B, :]).then_inc(norm_in[l], 16)
            for l, L in enumerate(layers):
                for k, (name, n) in enumerate((("wqkv", 3 * C), ("wproj", C), ("wfc1", HID), ("wfc2", 0))):
                    j = 4 * l + k
                    if j:
                        sp.wait_ge(made, 1 + j)
                    if k == 0:
                        for i, (bias, m) in enumerate((("bqkv", 3 * C), ("bproj", C), ("bfc2", C))):
                            o = (0, 3 * C, 4 * C)[i]
                            sp.dma_start(row[:, o:o + m], L[bias].rearrange("(a c) -> a c", a=1)).then_inc(w_in[j], 16)
                        bv = L["bqkv"].rearrange("(c a) -> c a", a=1)
                        sp.dma_start(vcol[:, 0:1], bv[2 * C + CB:3 * C, :]).then_inc(w_in[j], 16)
                        sp.dma_start(vcol[0:CB, 1:2], bv[2 * C:2 * C + CB, :]).then_inc(w_in[j], 16)
                    if k == 2:
                        sp.dma_start(b_fc1[l][:, :], L["bfc1"].rearrange("(m p) -> p m", p=128),
                                     allow_slow_non_contiguous=True).then_inc(w_in[j], 16)
                    if n:
                        sp.dma_start(stage[:, 0, 0:n], L[name][A, :]).then_inc(w_in[j], 16)
                        sp.dma_start(stage[0:CB, 1, 0:n], L[name][B, :]).then_inc(w_in[j], 16)
                        sp.dma_start(stage[CB:128, 1, 0:n], L[name][B, :]).then_inc(w_in[j], 16)
                    else:
                        sp.dma_start(stage[:, :, :].rearrange("p a n -> p (a n)")[:, 0:HC * C]
                                     .rearrange("p (m c) -> p m c", m=HC),
                                     L[name].rearrange("(m p) c -> p m c", p=128)).then_inc(w_in[j], 16)
            def next_image(it):
                sp.wait_ge(x_ordered, 2 * it + 2)
                following = (it + 1) % IMAGES
                sp.dma_start(x_img[:, :, :], x[following if isinstance(it, int) else sp.snap(following)]
                             .rearrange("(k p) h w -> p k (h w)", k=2)).then_inc(x_loaded, 16)

            def store(image):
                sp.dma_start(out[image].rearrange("(k p) h w -> p k (h w)", k=2), y_img[:, :, :])\
                    .then_inc(y_stored, 16)

            next_image(0)
            with sp.Fori(1, IMAGES) as it:
                next_image(it)
                when(sp, it, "y_ready", GROUP - 1)
                store(sp.snap(it - 1))
            when(sp, IMAGES - 1, "y_ready", TILES + GROUP - 1)
            store(IMAGES - 1)
            sp.wait_ge(y_stored, 16 * (IMAGES + 1))
            sp.wait_ge(x_loaded, 16 * (IMAGES + 1))

        W_DMAS = [8, 3, 4, 1]

        @block.tensor
        def _(pe):
            mm = nc.tensor.matmul
            for name in ("tr1", "qk_mm", "v_mm", "tqk", "s_mm", "shift", "tp", "pv", "to", "pr", "tr2", "fc1", "fc2",
                         "xtr", "otr"):
                pe.sem_inc(S[name], CREDIT)

            for l in range(LAYERS):
                sA1, sB1 = cols[:, l, 1, 0:1], cols[0:CB, l, 1, 1:2]
                sA2, sB2 = cols[:, l, 3, 0:1], cols[0:CB, l, 3, 1:2]
                pe.wait_ge(norm_in[l], 16 * 12)
                pe.wait_ge(w_in[4 * l], 16 * W_DMAS[0])
                pe.wait_ge(made, 1 + 4 * l)
                mm(ps_qk[0:1, 0:2 * C], sA1, stage[:, 0, 0:2 * C], start=True, stop=False)
                mm(ps_qk[0:1, 0:2 * C], sB1, stage[0:CB, 1, 0:2 * C], start=False, stop=True)
                for j, cs in enumerate((slice(2 * C + CB, 3 * C), slice(2 * C, 2 * C + CB))):
                    m = cs.stop - cs.start
                    mm(ps_v[0:m, j:j + 1], stage[:, 0, cs], sA1, start=True, stop=False)
                    last = mm(ps_v[0:m, j:j + 1], stage[0:CB, 1, cs], sB1, start=False, stop=True)
                last.then_inc(folded, 1)
                pe.wait_ge(w_in[4 * l + 1], 16 * W_DMAS[1])
                pe.wait_ge(made, 2 + 4 * l)
                mm(ps_o[0:1, 0:C], vcol[:, 0:1], stage[:, 0, 0:C], start=True, stop=False)
                mm(ps_o[0:1, 0:C], vcol[0:CB, 1:2], stage[0:CB, 1, 0:C], start=False, stop=True).then_inc(folded, 1)
                pe.wait_ge(w_in[4 * l + 2], 16 * W_DMAS[2])
                for m in range(HC):
                    cs = slice(m * 128, (m + 1) * 128)
                    mm(ps_s[:, 0, m:m + 1], stage[:, 0, cs], sA2, start=True, stop=False)
                    last = mm(ps_s[:, 0, m:m + 1], stage[0:CB, 1, cs], sB2, start=False, stop=True)
                last.then_inc(folded, 1)
                pe.wait_ge(made, 3 + 4 * l)
                mm(ps_t[:, 0, 0:2 * C], ones_row[:, :], rowsum[:, :], start=True, stop=True).then_inc(folded, 1)
            pe.wait_ge(made, 1 + 4 * LAYERS)
            pe.wait_ge(tables, 1)


            def slot(it, s, live):
                def ge(name, n):
                    when(pe, it, name, n)

                def take_tr(reader, n):
                    ge(*tr_reader)
                    tr_reader[:] = [reader, n]

                def contract(dst, w, lhs_tile, n0, n1, first=True):
                    for i, (blk, part) in enumerate(((0, 0), (2, 0), (0, 1), (1, 2), (1, 3))):
                        last = mm(dst, lhs_tile(blk), w[:, part, n0:n1], start=(first and i == 0), stop=(i == 4))
                    return last

                def transpose3(dst16, src):
                    nc.tensor.transpose(dst16[:, 0:TOK], src[:, 0, A], ident16[:, :])
                    for part in range(2):
                        nc.tensor.transpose(dst16[part * CB:(part + 1) * CB, TOK:2 * TOK], src[:, part, B], ident16[:, :])
                    return nc.tensor.transpose(dst16[:, 2 * TOK:3 * TOK], src[:, 1, A], ident16[:, :])

                def x_transpose(n):
                    layer, t = visit(n)
                    take_tr("x_in", visit_in_layer(n))
                    if t % GROUP == 0:
                        pe.wait_ge(x_ordered, 2 * (it + (n + GROUP) // STEPS) + t // GROUP + 1)
                    for k in range(2):
                        last = nc.tensor.transpose(ps_tr[:, k * H2:(k + 1) * H2], x_win[:, k, t * TOK:(t + 1) * TOK],
                                                   ident[0:H2, 0:H2])
                    last.then_inc(S["xtr"], 1)

                def norm1_transpose(n):
                    take_tr("xt_done", n)
                    if s == FIRST:
                        ge("y_ready", -1)
                    ge("lo1", n)
                    transpose3(ps_tr16, xs[:, 0, n % 2]).then_inc(S["tr1"], 1)

                def qk_product(n):
                    layer, t = visit(n)
                    ge("resid1", n - 4)
                    ge("xt_done", n)
                    mm(ps_qk[:, 0:2 * C], ones16[:, :], b_qk[layer][:, :], start=True, stop=False)
                    contract(ps_qk[:, 0:2 * C], w_qkv[layer], lambda b: xt[:, n % 2, b, :], 0, 2 * C,
                             first=False).then_inc(S["qk_mm"], 1)

                def v_product(n):
                    layer, t = visit(n)
                    if in_v is not None:
                        ge("resid2", in_v)
                    else:
                        ge("v_lo", n - 1)
                    contract(ps_v[:, 0:C], w_qkv[layer], lambda b: xt[:, n % 2, b, :], 2 * C, 3 * C)\
                        .then_inc(S["v_mm"], 1)

                def qk_transpose(n):
                    ge("p_lo", n - 2)
                    ge("qk_lo", n)
                    for qk_half in range(2):
                        for g in range(PAIRS):
                            h = qk_half * HEADS + 2 * g
                            last = nc.tensor.transpose(ps_t16[qk_half][:, g * TOK:(g + 1) * TOK],
                                                       qk[:, n % 2, h:h + 2].rearrange("p h s d -> p (h s d)"),
                                                       ident16[:, :])
                    last.then_inc(S["tqk"], 1)

                def scores(n):
                    layer, t = visit(n)
                    p, place = mlp_phase(n)
                    if place == 0 and p >= -1:
                        ge("gelu", p * HC + HC - 1)
                    ge("exp_done", n - 1)
                    ge("q_evac", n)
                    ge("k_evac", n)
                    if layer == 0:
                        kind = 2 * (t // 2 == 3) + t % 2
                        for par in range(2):
                            for part in range(2):
                                mm(ps_s[:, par, 0:PAIRS * WIN], ident16[:, :], bias_tab[:, kind, part, par, :, :],
                                   start=(part == 0), stop=False, skip_group_check=True)
                    else:
                        pe.nop(nofuse=True)
                    for g in range(PAIRS):
                        for w in range(2):
                            for par in range(2):
                                rows = slice(par * 64, par * 64 + 64)
                                tok = slice(w * WIN, (w + 1) * WIN)
                                last = mm(ps_s[w * WIN:(w + 1) * WIN, par, g * WIN:(g + 1) * WIN],
                                          qt[rows, n % 2, g, tok], kt[rows, n % 2, g, tok],
                                          start=(layer == 1 and g == 0), stop=False, skip_group_check=True)
                    last.then_inc(S["s_mm"], 1)

                def shift_scores(n):
                    ge("max_done", n)
                    for par in range(2):
                        last = mm(ps_s[:, par, 0:PAIRS * WIN].rearrange("p (g k) -> p g k", g=PAIRS), neg_ident[:, :],
                                  smax[:, n % 2, par, :].unsqueeze(2).broadcast_to([128, PAIRS, WIN]),
                                  start=False, stop=True, skip_group_check=True)
                    last.then_inc(S["shift"], 1)

                def p_transpose(n):
                    if not live(n + 1):
                        ge("p_lo", n - 1)
                    ge("exp_done", n)
                    for g in range(PAIRS):
                        last = nc.tensor.transpose(ps_t[:, g // 3, (g % 3) * TOK:(g % 3 + 1) * TOK],
                                                   p_tok[:, n % 2, g].rearrange("p a k -> p (a k)"), ident[:, :])
                    last.then_inc(S["tp"], 1)

                def pv_product(n):
                    ge("ot_done", n - 1)
                    ge("v_lo", n)
                    ge("p_lo", n)
                    for g in range(PAIRS):
                        for i, (ps, vs) in enumerate(((0, 0), (0, 1), (1, 0))):
                            last = mm(ps_o[:, g * 4 * VW:(g + 1) * 4 * VW], pt[:, n % 2, ps, g, :],
                                      v_blk[:, n % 2, vs, g].rearrange("p a w d -> p (a w d)"),
                                      start=(i == 0), stop=(i == 2))
                    last.then_inc(S["pv"], 1)

                def o_transpose(n):
                    q, at = mlp_phase(s - 1)
                    if q >= -1 and at == 1:
                        ge("resid2", q * GROUP + 1)
                    ge("o_lo", n)
                    transpose3(ps_o16, os[:, n % 2]).then_inc(S["to"], 1)

                def projection(n):
                    layer, t = visit(n)
                    if live(n + 3):
                        ge("qk_lo", n + 3)
                    else:
                        ge("resid1", n - 1)
                    ge("ot_done", n)
                    contract(ps_qk[:, 0:C], w_proj[layer], lambda b: ot[:, n % 2, b, :], 0, C)\
                        .then_inc(S["pr"], 1)

                def norm2_transpose(n):
                    take_tr("ht_done", n)
                    ge("lo2", n)
                    transpose3(ps_tr16, xs[:, 1, n % 2]).then_inc(S["tr2"], 1)

                def hidden(m):
                    layer, _ = visit(p * GROUP)
                    u = p * HC + m
                    if m == 0:
                        ge("ht_done", p * GROUP + GROUP - 1)
                        ge("exp_done", min(s - 1, end))
                    if m >= 2:
                        ge("gelu", u - 2)
                    for i, (part, blk) in enumerate(((0, 0), (0, 2), (1, 0), (2, 1), (3, 1))):
                        last = mm(ps_s[:, u % 2, :], w_fc1[layer][:, part, m * 128:(m + 1) * 128],
                                  ht[:, p % 2, blk, :], start=(i == 0), stop=(i == 4))
                    last.then_inc(S["fc1"], 1)

                def mlp_out(n, bank):
                    layer, t = visit(n)
                    tok = slice((t % GROUP) * TOK, (t % GROUP + 1) * TOK)
                    if n % GROUP == 0:
                        ge("h_hi", p * HC + HC - 1)
                        ge("h_lo", p * HC + HC - 1)
                    for m in range(HC):
                        for i, (hs, ws) in enumerate(((0, 0), (0, 1), (1, 0))):
                            last = mm(bank[:, 0:C], hid16[:, hs, m, tok], w_fc2[layer][:, ws, m, :],
                                      start=(m == 0 and i == 0), stop=(m == HC - 1 and i == 2))
                    last.then_inc(S["fc2"], 1)

                def y_transpose(n):
                    layer, t = visit(n)
                    take_tr("y_ready", visit_in_layer(n))
                    ge("resid2", n)
                    for k in range(2):
                        last = nc.tensor.transpose(ps_tr[0:H2, k * TOK:(k + 1) * TOK], x_tok[:, t, k * H2:(k + 1) * H2],
                                                   ident[:, :])
                    last.then_inc(S["otr"], 1)

                p, place = mlp_phase(s)
                end = STEPS + GROUP - 1
                mlp = p >= -1
                hid_slot, out_slot = mlp and place == 0, mlp and place > 0
                in_v = p * GROUP + (0, 0, 2, 3)[place] if out_slot else None
                last_block = out_slot and visit(p * GROUP)[0] == 1
                x_due = live(s + 4) and visit(s + 4)[0] == 0
                if live(s):
                    qk_product(s)
                if live(s + 1):
                    norm1_transpose(s + 1)
                if hid_slot:
                    hidden(0)
                    hidden(1)
                if out_slot:
                    ge("v_lo", min(s - 1, end))
                    if s - 1 > end:
                        ge("resid2", in_v - 1)
                    mlp_out(in_v, ps_v)
                    if last_block and place == 2:
                        y_transpose(p * GROUP + 1)
                if live(s - 3):
                    o_transpose(s - 3)
                if live(s):
                    qk_transpose(s)
                if live(s - 2):
                    pv_product(s - 2)
                if hid_slot:
                    for m in range(2, HC):
                        if m == 4 and live(s - 4):
                            norm2_transpose(s - 4)
                        hidden(m)
                if x_due:
                    x_transpose(s + 4)
                if live(s - 3):
                    projection(s - 3)
                if live(s):
                    scores(s)
                    v_product(s)
                if not hid_slot:
                    if live(s - 4):
                        norm2_transpose(s - 4)
                if live(s - 1):
                    p_transpose(s - 1)
                if out_slot and place == 1:
                    ge("o_evac", min(s - 2, end))
                    if s - 2 > end:
                        ge("ot_done", end)
                    mlp_out(p * GROUP + 1, ps_o)
                if last_block:
                    y_transpose(p * GROUP + place - (place == 1))
                if live(s):
                    shift_scores(s)

            tr_reader = ["x_in", -1]
            run(pe, slot)

        @block.scalar
        def _(act):
            copy = nc.scalar.activation
            for name in ("x_in", "xt_done", "hi1", "qk_hi", "v_hi", "k_evac", "exp_done", "p_hi", "o_evac", "o_hi",
                         "hi2", "ht_done", "gelu", "y_ready", "exp_loaded"):
                act.sem_inc(S[name], CREDIT)
            act.wait_ge(made, 1 + 4 * LAYERS)

            def slot(it, s, live):
                def ge(name, n):
                    when(act, it, name, n)

                def x_evac(n):
                    ge("xtr", visit_in_layer(n))
                    copy(stream(n, 0), ps_tr[:, 0:C], ACT.Copy).then_inc(S["x_in"], 1)

                def norm_hi(n, which):
                    a = "12"[which]
                    ge("ln" + a, n)
                    ge("tr" + a, n - 2)
                    copy(xs[:, which, n % 2, 0, :], xn[:, which, n % 2, :], ACT.Copy).then_inc(S["hi" + a], 1)

                def xt_evac(n):
                    ge("tr1", n)
                    copy(xt[:, n % 2].rearrange("p b t -> p (b t)"), ps_tr16[:, 0:3 * TOK], ACT.Copy)\
                        .then_inc(S["xt_done"], 1)

                def ht_evac(n):
                    ge("tr2", n)
                    copy(ht[:, n // GROUP % 2, :, (n % GROUP) * TOK:(n % GROUP + 1) * TOK],
                         ps_tr16[:, 0:3 * TOK].rearrange("p (b t) -> p b t", b=3), ACT.Copy).then_inc(S["ht_done"], 1)

                def qk_hi(n):
                    ge("qk_mm", n)
                    for i, places in enumerate((slice(0, 2), slice(0, 3, 2))):
                        src = ps_qk[:, i * C:(i + 1) * C].rearrange("p (h d) -> p h d", d=HD).unsqueeze(2)
                        last = copy(qk[:, n % 2, i * HEADS:(i + 1) * HEADS, places, :],
                                    src.broadcast_to([128, HEADS, 2, HD]), ACT.Copy, scale=UNSCALE)
                    last.then_inc(S["qk_hi"], 1)

                def v_hi(n):
                    ge("v_mm", n)
                    for par in range(2):
                        for w in range(2):
                            src, dst = v_places(n, par, w, 0)
                            last = copy(dst, src, ACT.Copy, scale=UNSCALE)
                    last.then_inc(S["v_hi"], 1)

                def k_evac(n):
                    ge("tqk", n)
                    copy(kt[:, n % 2].rearrange("p g t -> p (g t)"), ps_t16[1][:, 0:PAIRS * TOK], ACT.Copy)\
                        .then_inc(S["k_evac"], 1)

                def exp(n):
                    ge("shift", n)
                    nc.scalar.activation(p_tok[:, n % 2].rearrange("p g a k -> p a g k"),
                                         ps_s[:, :, 0:PAIRS * WIN].rearrange("p a (g k) -> p a g k", g=PAIRS),
                                         ACT.Exp).then_inc(S["exp_done"], 1)

                def p_hi(n):
                    ge("tp", n)
                    copy(pt[:, n % 2, 0].rearrange("p (b g) t -> p b (g t)", b=2), ps_t[:, :, 0:3 * TOK], ACT.Copy)\
                        .then_inc(S["p_hi"], 1)

                def o_evac(n):
                    ge("pv", n)
                    for w in range(2):
                        rows = slice(w * WIN, (w + 1) * WIN)
                        src = ps_o[rows, 0:4 * PAIRS * VW].rearrange("p (h w d) -> p h w d", w=2, d=VW)[:, :, w]
                        last = copy(o_raw[rows, n % 2], src, ACT.Copy)
                    last.then_inc(S["o_evac"], 1)

                def o_hi(n):
                    ge("o_norm", n)
                    copy(os[:, n % 2, 0, :], o_tok[:, n % 2, :], ACT.Copy).then_inc(S["o_hi"], 1)

                def gelu(m):
                    layer, _ = visit(p * GROUP)
                    u = p * HC + m
                    ge("fc1", u)
                    ge("h_hi", u - 2)
                    ge("h_lo", u - 2)
                    nc.scalar.activation(hid[:, u % 2, :], ps_s[:, u % 2, :], ACT.Gelu, bias=b_fc1[layer][:, m:m + 1],
                                         scale=UNSCALE).then_inc(S["gelu"], 1)

                def load_exp():
                    ge("exp_loaded", p - 1)
                    nc.scalar.activation(spare[:, :], half[0:1, :], ACT.Exp).then_inc(S["exp_loaded"], 1)

                def y_evac(n):
                    layer, t = visit(n)
                    ge("otr", visit_in_layer(n))
                    if t == 0:
                        act.wait_ge(y_stored, it * 16 + 16)
                    tile = ps_tr[0:H2, 0:2 * TOK].rearrange("p (k t) -> p k t", k=2)
                    for win, img in box_pairs(t, tile, y_img[:, :, :]):
                        last = copy(img, win, ACT.Copy)
                    last.then_inc(S["y_ready"], 1)

                p, place = mlp_phase(s)
                mlp = p >= -1
                hid_slot = mlp and place == 0
                last_block = mlp and place and visit(p * GROUP)[0] == 1
                x_due = live(s + 4) and visit(s + 4)[0] == 0
                if live(s):
                    qk_hi(s)
                if live(s + 1):
                    xt_evac(s + 1)
                if hid_slot:
                    gelu(0)
                if live(s - 4) and hid_slot:
                    norm_hi(s - 4, 1)
                if last_block and place == 2:
                    y_evac(p * GROUP + 1)
                if hid_slot:
                    gelu(1)
                if live(s):
                    k_evac(s)
                if hid_slot:
                    gelu(2)
                if live(s - 2):
                    o_evac(s - 2)
                if live(s - 4) and not hid_slot:
                    norm_hi(s - 4, 1)
                if hid_slot:
                    gelu(3)
                    if live(s - 4):
                        ht_evac(s - 4)
                    gelu(4)
                    gelu(5)
                if x_due:
                    x_evac(s + 4)
                if live(s + 2):
                    norm_hi(s + 2, 0)
                if hid_slot:
                    load_exp()
                if live(s):
                    v_hi(s)
                if not hid_slot:
                    if live(s - 4):
                        ht_evac(s - 4)
                if live(s - 1):
                    p_hi(s - 1)
                if last_block:
                    y_evac(p * GROUP + place - (place == 1))
                if live(s):
                    exp(s)
                if live(s - 2):
                    o_hi(s - 2)

            run(act, slot)

        @block.vector
        def _(dve):
            v = nc.vector
            for name in ("bn1a", "bn1", "qk_lo", "v_lo", "q_evac", "max_done", "p_lo", "inv_done",
                         "ot_done", "resid1", "bn2a", "bn2", "lo2", "h_lo", "resid2"):
                dve.sem_inc(S[name], CREDIT)

            steps = [0]

            def link(ins):
                steps[0] += 1
                ins.then_inc(dve_chain, 1)
                dve.wait_ge(dve_chain, steps[0])

            v.memset(ones16[:, :], 1.0)
            v.memset(ones_row[:, :], 1.0)
            v.memset(half[:, :], -0.5)
            v.memset(x_tok[:, :, :].rearrange("p t c -> p (t c)"), 0.0)
            for l in range(LAYERS):
                v.memset(b_qk[l][:, :], 0.0)
            v.memset(qk[:, :].rearrange("p r h s d -> p (r h s d)"), 0.0)
            link(v.memset(v_blk[:, :].rearrange("p r s g a w d -> p (r s g a w d)"), 0.0))
            for par in range(2):
                for r in range(2):
                    v.memset(v_blk[par * 64:par * 64 + 64, r, 0, :, par, :, HD:VW], 1.0)
            dve.wait_ge(const_in[0], 16)
            link(v.tensor_copy(ident16[:, :], ident[:, :]))
            v.tensor_scalar(neg_ident[:, :], ident[:, :], -1.0, None, ALU.mult).then_inc(made, 1)

            def split(hi, lo, src):
                link(v.tensor_copy(hi, src))
                link(v.tensor_tensor(lo, src, hi, ALU.subtract))

            def make_weight(w, n, gain, q_cols=0):
                for ab in range(2):
                    for c0, c1, s in ((0, q_cols, WSCALE * QSCALE), (q_cols, n, WSCALE)):
                        if c1 > c0:
                            src, dst = stage[:, ab, c0:c1], scaled[:, ab, c0:c1]
                            if gain is None:
                                link(v.tensor_scalar(dst, src, s, None, ALU.mult))
                            else:
                                link(v.tensor_scalar(dst, src, gain[:, ab:ab + 1], s, ALU.mult, ALU.mult))
                    split(w[:, 2 * ab, 0:n], w[:, 2 * ab + 1, 0:n], scaled[:, ab, 0:n])

            for l in range(LAYERS):
                dve.wait_ge(norm_in[l], 16 * 12)
                dve.wait_ge(w_in[4 * l], 16 * W_DMAS[0])
                make_weight(w_qkv[l], 3 * C, cols[:, l, 0, :], q_cols=C)
                dve.wait_ge(folded, 4 * l + 1)
                link(v.tensor_tensor(row[:, 0:2 * C], row[:, 0:2 * C], ps_qk[0:1, 0:2 * C], ALU.add))
                link(v.tensor_scalar(row[:, 0:C], row[:, 0:C], WSCALE * QSCALE, None, ALU.mult))
                link(v.tensor_scalar(row[:, C:2 * C], row[:, C:2 * C], WSCALE, None, ALU.mult))
                split(b_qk[l][0:1, :], b_qk[l][32:33, :], row[:, 0:2 * C])
                link(v.tensor_tensor(vcol[:, 0:1], vcol[:, 0:1], ps_v[:, 0:1], ALU.add))
                v.tensor_tensor(vcol[0:CB, 1:2], vcol[0:CB, 1:2], ps_v[0:CB, 1:2], ALU.add).then_inc(made, 1)
                dve.wait_ge(w_in[4 * l + 1], 16 * W_DMAS[1])
                make_weight(w_proj[l], C, None)
                dve.wait_ge(folded, 4 * l + 2)
                link(v.tensor_tensor(rowsum[:, 0:C], row[:, 3 * C:4 * C], ps_o[0:1, 0:C], ALU.add))
                v.tensor_copy(rowsum[:, C:2 * C], row[:, 4 * C:5 * C]).then_inc(made, 1)
                dve.wait_ge(w_in[4 * l + 2], 16 * W_DMAS[2])
                make_weight(w_fc1[l], HID, cols[:, l, 2, :])
                dve.wait_ge(folded, 4 * l + 3)
                v.tensor_tensor(b_fc1[l][:, :], b_fc1[l][:, :], ps_s[:, 0, 0:HC], ALU.add).then_inc(made, 1)
                dve.wait_ge(w_in[4 * l + 3], 16 * W_DMAS[3])
                flat = stage[:, :, :].rearrange("p a n -> p (a n)")[:, 0:HC * C]
                flat2 = scaled[:, :, :].rearrange("p a n -> p (a n)")[:, 0:HC * C]
                link(v.tensor_scalar(flat2, flat, WSCALE, None, ALU.mult))
                split(w_fc2[l][:, 0].rearrange("p m c -> p (m c)"), w_fc2[l][:, 1].rearrange("p m c -> p (m c)"), flat2)
                dve.wait_ge(folded, 4 * l + 4)
                link(v.tensor_copy(b_proj[l][:, :], ps_t[:, 0, 0:C]))
                v.tensor_copy(b_fc2[l][:, :], ps_t[:, 0, C:2 * C]).then_inc(made, 1)
            dve.wait_ge(const_in[2], 16 * 2 * WS)
            for key in range(WIN):
                last = v.tensor_copy(rel_t[:, :, :, key], rel[:, WIN - 1 - key, :].rearrange("p (g a) -> p a g", a=2))
            link(last)
            dve.wait_ge(const_in[1], 16)
            for kind in range(4):
                for par in range(2):
                    link(v.tensor_tensor(rel_m[:, par], rel_t[:, par],
                                         mask[:, kind, :].unsqueeze(1).broadcast_to([128, PAIRS, WIN]), ALU.add))
                link(v.tensor_copy(bias_tab[:, kind, 0], rel_m[:, :]))
                last = v.tensor_tensor(bias_tab[:, kind, 1], rel_m[:, :], bias_tab[:, kind, 0], ALU.subtract)
                if kind < 3:
                    link(last)
            last.then_inc(tables, 1)

            def slot(it, s, live):
                def ge(name, n):
                    when(dve, it, name, n)

                def statistics(n, which):
                    a = "12"[which]
                    layer, _ = visit(n)
                    if which == 1:
                        ge("resid1", n)
                    elif layer == 0:
                        ge("x_in", visit_in_layer(n))
                    elif n >= STEPS - GROUP or s >= FIRST:
                        ge("resid2", n - 3 * GROUP)
                    v.bn_stats(bn6[:, which, n % 2, :], stream(n, which)).then_inc(S[f"bn{a}a"], 1)

                def mean_variance(n, which):
                    a = "12"[which]
                    ge(f"bn{a}a", n)
                    ge("ln" + a, n - 2)
                    dve.nop(nofuse=True)
                    v.bn_aggr(mv[:, which, n % 2, :], bn6[:, which, n % 2, :]).then_inc(S["bn" + a], 1)

                def norm_lo(n):
                    ge("hi2", n)
                    v.tensor_tensor(xs[:, 1, n % 2, 1, :], xn[:, 1, n % 2, :], xs[:, 1, n % 2, 0, :],
                                    ALU.subtract).then_inc(S["lo2"], 1)

                def qk_lo(n):
                    ge("qk_hi", n)
                    for i, place in enumerate((2, 1)):
                        heads = slice(i * HEADS, (i + 1) * HEADS)
                        last = v.scalar_tensor_tensor(
                            out=qk[:, n % 2, heads, place, :],
                            in0=ps_qk[:, i * C:(i + 1) * C].rearrange("p (h d) -> p h d", d=HD), scalar=UNSCALE,
                            in1=qk[:, n % 2, heads, 0, :], op0=ALU.mult, op1=ALU.subtract)
                    last.then_inc(S["qk_lo"], 1)

                def v_lo(n):
                    ge("v_hi", n)
                    for par in range(2):
                        for w in range(2):
                            src, dst = v_places(n, par, w, 1)
                            last = v.scalar_tensor_tensor(out=dst, in0=src, scalar=UNSCALE,
                                                          in1=v_places(n, par, w, 0)[1],
                                                          op0=ALU.mult, op1=ALU.subtract)
                    last.then_inc(S["v_lo"], 1)

                def q_evac(n):
                    ge("tqk", n)
                    v.tensor_copy(qt[:, n % 2].rearrange("p g t -> p (g t)"), ps_t16[0][:, 0:PAIRS * TOK])\
                        .then_inc(S["q_evac"], 1)

                def row_max(n):
                    ge("s_mm", n)
                    v.tensor_reduce(smax[:, n % 2], ps_s[:, :, 0:PAIRS * WIN].rearrange("p a (g k) -> p a g k", g=PAIRS),
                                    AX.X, ALU.max).then_inc(S["max_done"], 1)

                def p_lo(n):
                    ge("p_hi", n)
                    v.tensor_tensor(pt[:, n % 2, 1].rearrange("p (b g) t -> p b (g t)", b=2), ps_t[:, :, 0:3 * TOK],
                                    pt[:, n % 2, 0].rearrange("p (b g) t -> p b (g t)", b=2), ALU.subtract)\
                        .then_inc(S["p_lo"], 1)

                def inverse_sums(n):
                    ge("o_evac", n)
                    v.reciprocal(o_inv[:, n % 2, :], o_raw[:, n % 2, :, HD]).then_inc(S["inv_done"], 1)

                def ot_evac(n):
                    ge("to", n)
                    v.tensor_copy(ot[:, n % 2].rearrange("p b t -> p (b t)"), ps_o16[:, 0:3 * TOK])\
                        .then_inc(S["ot_done"], 1)

                def residual(n, src, out, old, product, bias, done):
                    ge(product, n)
                    ge(bias, n)
                    v.scalar_tensor_tensor(out=out, in0=src, scalar=UNSCALE, in1=old,
                                           op0=ALU.mult, op1=ALU.add).then_inc(S[done], 1)

                def attention_residual(n):
                    residual(n, ps_qk[:, 0:C], stream(n, 1), stream(n, 0), "pr", "bias1", "resid1")

                def mlp_residual(n, bank):
                    residual(n, bank[:, 0:C], x_tok[:, visit(n)[1], :], stream(n, 1), "fc2", "bias2", "resid2")

                def hidden_lo(m):
                    u = p * HC + m
                    ge("gelu", u)
                    ge("h_hi", u)
                    v.tensor_tensor(hid16[:, 1, m, :], hid[:, u % 2, :], hid16[:, 0, m, :], ALU.subtract)\
                        .then_inc(S["h_lo"], 1)

                p, place = mlp_phase(s)
                mlp = p >= -1
                hid_slot = mlp and place == 0
                if live(s):
                    qk_lo(s)
                if mlp and place:
                    mlp_residual(p * GROUP + (0, 0, 2, 3)[place], ps_v)
                if live(s - 3):
                    ot_evac(s - 3)
                if live(s):
                    q_evac(s)
                if live(s - 4) and hid_slot:
                    norm_lo(s - 4)
                if hid_slot:
                    hidden_lo(0)
                    hidden_lo(1)
                    hidden_lo(2)
                if live(s - 2):
                    inverse_sums(s - 2)
                if hid_slot:
                    hidden_lo(3)
                    hidden_lo(4)
                if live(s - 3):
                    attention_residual(s - 3)
                if live(s - 4) and not hid_slot:
                    norm_lo(s - 4)
                if live(s):
                    row_max(s)
                if hid_slot:
                    hidden_lo(5)
                if live(s):
                    v_lo(s)
                if live(s - 1):
                    p_lo(s - 1)
                if mlp and place == 1:
                    mlp_residual(p * GROUP + 1, ps_o)
                for n, which in ((s - 3, 1), (s + 3, 0)):
                    if live(n):
                        statistics(n, which)
                for n, which in ((s - 3, 1), (s + 3, 0)):
                    if live(n):
                        mean_variance(n, which)

            run(dve, slot)

        @block.gpsimd
        def _(pool):
            g_ = nc.gpsimd
            for name in ("ln1a", "ln1b", "ln1", "bias1", "o_norm", "o_lo", "lo1", "ln2a", "ln2b", "ln2", "bias2", "h_hi"):
                pool.sem_inc(S[name], CREDIT)

            def order_tile(t):
                for win, img in box_pairs(t, x_win[:, :, t * TOK:(t + 1) * TOK], x_img[:, :, :]):
                    last = g_.tensor_scalar(win, img, 1.0, 0.0, ALU.mult, ALU.add)
                if t % GROUP == GROUP - 1:
                    last.then_inc(x_ordered, 1)

            def order_half(it, half):
                when(pool, it, "xtr", half * GROUP + GROUP - 1)
                if half == 0:
                    pool.wait_ge(x_loaded, it * 16 + 32)
                pool.nop(nofuse=True)
                for t in range(half * GROUP, (half + 1) * GROUP):
                    order_tile(t)

            pool.wait_ge(x_loaded, 16)
            for t in range(TILES):
                order_tile(t)
            pool.wait_ge(made, 1 + 4 * LAYERS)

            def slot(it, s, live):
                def ge(name, n):
                    when(pool, it, name, n)

                def scale(n, which):
                    a, r = "12"[which], n % 2
                    ge("bn" + a, n)
                    pool.nop(nofuse=True)
                    g_.tensor_scalar(nmean[:, which, r:r + 1], mv[:, which, r, 0:1], -1.0, 0.0, ALU.mult, ALU.add)
                    g_.tensor_scalar(vare[:, which, r:r + 1], mv[:, which, r, 1:2], EPS, 1.0, ALU.add, ALU.mult)\
                        .then_inc(S[f"ln{a}a"], 1)
                    ge(f"ln{a}a", n)
                    g_.tensor_tensor(rstd[:, which, r:r + 1], vare[:, which, r:r + 1], half[:, :], ALU.pow)\
                        .then_inc(S[f"ln{a}b"], 1)

                def apply(n, which):
                    a, r = "12"[which], n % 2
                    ge(f"ln{a}b", n)
                    ge("lo" + a, n - 2)
                    pool.nop(nofuse=True)
                    g_.tensor_scalar(xn[:, which, r, :], stream(n, which), nmean[:, which, r:r + 1],
                                     rstd[:, which, r:r + 1], ALU.add, ALU.mult).then_inc(S["ln" + a], 1)

                def add_bias(n, which):
                    bias = (b_proj, b_fc2)[which][visit(n)[0]]
                    g_.tensor_tensor(stream(n, which), stream(n, which), bias[:, :], ALU.add)\
                        .then_inc(S["bias" + "12"[which]], 1)

                def o_norm(n):
                    ge("inv_done", n)
                    g_.tensor_tensor(o_tok[:, n % 2, :].rearrange("p (h d) -> p h d", d=HD), o_raw[:, n % 2, :, 0:HD],
                                     o_inv[:, n % 2, :].unsqueeze(2).broadcast_to([128, HEADS, HD]), ALU.mult)\
                        .then_inc(S["o_norm"], 1)

                def o_lo(n):
                    ge("o_hi", n)
                    g_.tensor_tensor(os[:, n % 2, 1, :], o_tok[:, n % 2, :], os[:, n % 2, 0, :], ALU.subtract)\
                        .then_inc(S["o_lo"], 1)

                def norm1_lo(n):
                    ge("hi1", n)
                    g_.tensor_tensor(xs[:, 0, n % 2, 1, :], xn[:, 0, n % 2, :], xs[:, 0, n % 2, 0, :],
                                     ALU.subtract).then_inc(S["lo1"], 1)

                def hidden_hi(m):
                    u = p * HC + m
                    ge("gelu", u)
                    pool.nop(nofuse=True)
                    g_.tensor_scalar(hid16[:, 0, m, :], hid[:, u % 2, :], 1.0, 0.0, ALU.mult, ALU.add)\
                        .then_inc(S["h_hi"], 1)

                p, place = mlp_phase(s)
                hid_slot = p >= -1 and place == 0
                if live(s - 4):
                    scale(s - 4, 1)
                    apply(s - 4, 1)
                    add_bias(s - 4, 1)
                if hid_slot:
                    hidden_hi(0)
                    hidden_hi(1)
                if live(s + 2):
                    scale(s + 2, 0)
                if hid_slot:
                    hidden_hi(2)
                if live(s + 2):
                    apply(s + 2, 0)
                if hid_slot:
                    hidden_hi(3)
                if live(s + 2):
                    add_bias(s + 2, 0)
                if hid_slot:
                    hidden_hi(4)
                    hidden_hi(5)
                if live(s - 2):
                    o_norm(s - 2)
                if live(s + 2):
                    norm1_lo(s + 2)
                if s in (FIRST, FIRST + 2 * GROUP):
                    order_half(it, (s - FIRST) // (2 * GROUP))
                if live(s - 2):
                    o_lo(s - 2)

            run(pool, slot)


_BLOCKS = [
    {"wqkv": "L0_conv_qkv_w", "bqkv": "L0_conv_qkv_b", "wproj": "L0_conv_proj_w", "bproj": "L0_conv_proj_b",
     "g1": "L0_conv_norm1_g", "b1": "L0_conv_norm1_b", "g2": "L0_conv_norm2_g", "b2": "L0_conv_norm2_b",
     "wfc1": "L0_conv_fc1_w", "bfc1": "L0_conv_fc1_b", "wfc2": "L0_conv_fc2_w", "bfc2": "L0_conv_fc2_b"},
    {"wqkv": "L1_conv_w_qkv", "bqkv": "L1_conv_b_qkv", "wproj": "L1_conv_w_proj", "bproj": "L1_conv_b_proj",
     "g1": "L1_conv_gamma1", "b1": "L1_conv_beta1", "g2": "L1_conv_gamma2", "b2": "L1_conv_beta2",
     "wfc1": "L1_conv_w_fc1", "bfc1": "L1_conv_b_fc1", "wfc2": "L1_conv_w_fc2", "bfc2": "L1_conv_b_fc2"},
]


def _constants(np):
    ident = np.eye(128, dtype=np.float32)
    mask = np.zeros((128, 4, WIN), np.float32)
    r, c = np.divmod(np.arange(WIN), WS)
    for kind in range(4):
        for w in range(2):
            apart = np.zeros((WIN, WIN), bool)
            if kind // 2:
                apart |= (r[:, None] < SHIFT) != (r[None] < SHIFT)
            if kind % 2 and w == 1:
                apart |= (c[:, None] < SHIFT) != (c[None] < SHIFT)
            mask[w * WIN:(w + 1) * WIN, kind] = np.where(apart, np.float32(-10.0), np.float32(0.0))
    return ident, mask


def kernel(**inputs):
    import numpy as _np
    import concourse.bacc as _bacc
    from concourse import mybir as _mybir
    from concourse.bass_utils import run_bass_kernel_spmd as _run

    nc = _bacc.Bacc("TRN2", target_bir_lowering=False, num_devices=1)
    ident, mask = _constants(_np)
    given = {k: inputs[k] for k in inputs} | {"const_ident": ident, "const_mask": mask}
    arrays, args = {}, {}
    for name, a in given.items():
        a = _np.ascontiguousarray(a)
        arrays[f"in_{name}_dram"] = a
        args[name] = nc.dram_tensor(f"in_{name}_dram", a.shape, _mybir.dt.from_np(a.dtype), kind="ExternalInput").ap()
    out = nc.dram_tensor("out_0_dram", (IMAGES, C, SIDE, SIDE), _mybir.dt.float32, kind="ExternalOutput").ap()
    layers = [{k: args[v] for k, v in b.items()} for b in _BLOCKS]
    swin_program(nc, args["x"], layers, args["L0_conv_rel_bias"], args["const_ident"], args["const_mask"], out)
    r = _run(nc, [arrays], core_ids=[0])
    return r.results[0]["out_0_dram"]
```

```python
from contextlib import ExitStack

import concourse.bass as bass
from concourse import mybir

F32 = mybir.dt.float32
F16 = mybir.dt.float16
BF16 = mybir.dt.bfloat16
ALU = mybir.AluOpType
ACT = mybir.ActivationFunctionType
AX = mybir.AxisListType

IMAGES, C, SIDE = 32, 192, 32
HEADS, HD = 12, 16
PAIRS = HEADS // 2
WS, SHIFT = 8, 4
WIN = WS * WS
TOK = 2 * WIN
TILES = SIDE * SIDE // TOK
LAYERS = 2
STEPS = LAYERS * TILES
GROUP = 4
PHASES = STEPS // GROUP
HID = 4 * C
HC = HID // 128
CB = 64
WSCALE = 64.0
UNSCALE = 1.0 / WSCALE
QSCALE = HD ** -0.5
VW = HD + 1
CREDIT = 4
FIRST, LAST = 4, 4 + STEPS
EPS = 1e-5
KINDS = 4
REGIONS = 4


def visit(n):
    layer, group = ((1, 1), (0, 1), (1, 0), (0, 0))[n // GROUP % PHASES]
    return layer, group * GROUP + n % GROUP


def visit_in_layer(n):
    layer, _ = visit(n)
    return (n + (0 if layer else GROUP)) // (2 * GROUP) * GROUP + n % GROUP


def mlp_phase(s):
    return (s - FIRST) // GROUP - 1, (s - FIRST) % GROUP


def window_pieces(t):
    i, jp = t // 2, t % 2
    rows = [(0, WS, WS * i + SHIFT)] if i < 3 else [(0, SHIFT, SIDE - SHIFT), (SHIFT, SHIFT, 0)]
    cols = [(0, 2, 0, WS, SHIFT)] if jp == 0 else [
        (0, 1, 0, WS, 2 * WS + SHIFT), (1, 1, 0, SHIFT, SIDE - SHIFT), (1, 1, SHIFT, SHIFT, 0)]
    return [(w0, nw, r0, nr, c0, nc, row, col) for r0, nr, row in rows for w0, nw, c0, nc, col in cols]


def box_pairs(t, tile_view, image_view):
    tv = tile_view.rearrange("p k (w r c) -> p k w r c", w=2, r=WS)
    iv = image_view.rearrange("p k (r c) -> p k r c", r=SIDE)
    out = []
    for w0, nw, r0, nr, c0, nc, row, col in window_pieces(t):
        if nw == 2:
            for k in range(2):
                out.append((tv[:, k, :, r0:r0 + nr, :],
                            iv[:, k, row:row + nr, col:col + 2 * WS].rearrange("p r (w c) -> p w r c", w=2)))
        else:
            out.append((tv[:, :, w0, r0:r0 + nr, c0:c0 + nc], iv[:, :, row:row + nr, col:col + nc]))
    return out


def swin_program(nc, x, layers, rel_bias, ident_in, q_mask_in, k_mask_in, out):
    H2 = C // 2
    with ExitStack() as ctx:
        def sb(name, shape, dt):
            return ctx.enter_context(nc.sbuf_tensor(name, shape, dt))

        def sem(name):
            return ctx.enter_context(nc.semaphore(name))

        banks = [ctx.enter_context(nc.psum_tensor(f"bank{i}", [128, 512], F32)) for i in range(4)]
        ps_s = ctx.enter_context(nc.psum_tensor("ps_s", [128, 2, 512], F32))
        ps_t = ctx.enter_context(nc.psum_tensor("ps_t", [128, 2, 512], F32))
        ps_tr, ps_o, ps_qk, ps_v = banks
        ps_tr16 = ps_tr[:, :].bitcast(F16)
        ps_o16 = ps_o[:, :].bitcast(F16)
        ps_t16 = [ps_t[:, i, :].bitcast(F16) for i in range(2)]

        ident = sb("ident", [128, 128], F32)
        ident16 = sb("ident16", [128, 128], F16)
        pair_ident = sb("pair_ident", [128, 128], F16)
        neg_ident = sb("neg_ident", [128, 128], BF16)
        ones_row = sb("ones_row", [1, 128], F32)
        q_mask = sb("q_mask", [128, REGIONS], F32)
        k_mask = sb("k_mask", [128, KINDS + 1, REGIONS], F32)
        rel = sb("rel", [128, WIN, HEADS], F32)
        rel_t = sb("rel_t", [128, 2, PAIRS, WIN], F32)
        bias_tab = sb("bias_tab", [128, 2, PAIRS, WIN], F16)
        stage = sb("stage", [128, 2, 2, HID], F32)
        scaled = sb("scaled", [128, 2, HID], F32)
        cols = sb("cols", [128, LAYERS, 4, 2], F32)
        vcol = sb("vcol", [128, 2], F32)
        row = sb("row", [1, 5 * C], F32)
        rowsum = sb("rowsum", [1, 2 * C], F32)
        w_qkv = [sb(f"w_qkv{l}", [128, 4, 3 * C], F16) for l in range(LAYERS)]
        w_proj = [sb(f"w_proj{l}", [128, 4, C], F16) for l in range(LAYERS)]
        w_fc1 = [sb(f"w_fc1{l}", [128, 4, HID], F16) for l in range(LAYERS)]
        w_fc2 = [sb(f"w_fc2{l}", [128, 2, HC, C], F16) for l in range(LAYERS)]
        row16 = sb("row16", [1, 2 * C], F16)
        b_proj = [sb(f"b_proj{l}", [128, C], F32) for l in range(LAYERS)]
        b_fc1 = [sb(f"b_fc1{l}", [128, HC], F32) for l in range(LAYERS)]
        b_fc2 = [sb(f"b_fc2{l}", [128, C], F32) for l in range(LAYERS)]

        x_img = sb("x_img", [H2, 2, SIDE * SIDE], F32)
        x_win = sb("x_win", [H2, 2, SIDE * SIDE], F32)
        y_img = sb("y_img", [H2, 2, SIDE * SIDE], F32)
        x_new = sb("x_new", [128, GROUP, C], F32)
        x_mid = sb("x_mid", [128, GROUP, C], F32)
        x_tok = sb("x_tok", [128, TILES, C], F32)
        bn6 = sb("bn6", [128, 2, 2, 6], F32)
        mv = sb("mv", [128, 2, 2, 2], F32)
        nmean = sb("nmean", [128, 2, 2], F32)
        vare = sb("vare", [128, 2, 2], F32)
        rstd = sb("rstd", [128, 2, 2], F32)
        half = sb("half", [128, 1], F32)
        spare = sb("spare", [1, 1], F32)
        xn = sb("xn", [128, 2, 2, C], F32)
        xs = sb("xs", [128, 2, 2, 2, C], F16)
        xt = sb("xt", [128, 2, 4, TOK], F16)
        ht = sb("ht", [128, 2, 3, GROUP * TOK], F16)
        qk = sb("qk", [128, 2, 2 * HEADS, 4, HD], F16)
        qt = sb("qt", [128, 2, PAIRS, TOK], F16)
        kt = sb("kt", [128, 2, PAIRS, TOK], F16)
        v_blk = sb("v_blk", [128, 2, 2, PAIRS, 2, 2, VW], F16)
        smax = sb("smax", [128, 2, 2, PAIRS], BF16)
        p_tok = sb("p_tok", [128, 2, PAIRS, 2, WIN], F32)
        pt = sb("pt", [128, 2, 2, PAIRS, TOK], F16)
        o_raw = sb("o_raw", [128, 2, HEADS, VW], F32)
        o_inv = sb("o_inv", [128, 2, HEADS], F32)
        o_tok = sb("o_tok", [128, 2, C], F32)
        os = sb("os", [128, 2, 2, C], F16)
        ot = sb("ot", [128, 2, 3, TOK], F16)
        hid = sb("hid", [128, 2, GROUP * TOK], F32)
        hid16 = sb("hid16", [128, 2, HC, GROUP * TOK], F16)

        const_in = [sem(f"const_in{i}") for i in range(3)]
        norm_in = [sem(f"norm_in{l}") for l in range(LAYERS)]
        w_in = [sem(f"w_in{j}") for j in range(4 * LAYERS)]
        folded = sem("folded")
        made = sem("made")
        dve_chain = sem("dve_chain")
        tables = sem("tables")
        pool_chain = sem("pool_chain")

        COUNT = {name: STEPS for name in (
            "bn1a bn1 ln1a ln1b ln1 bias1 hi1 lo1 tr1 xt_done qk_mm v_mm mask_set qk_hi qk_lo v_hi v_lo tqk q_evac "
            "k_evac s_mm max_done shift exp_done tp p_hi p_lo pv o_evac inv_done o_norm o_hi o_lo to ot_done "
            "pr resid1 bn2a bn2 ln2a ln2b ln2 bias2 hi2 lo2 tr2 ht_done fc2 resid2").split()}
        AHEAD = dict.fromkeys(COUNT, GROUP)
        COUNT |= {name: PHASES * HC for name in ("fc1", "gelu", "h_hi", "h_lo")}
        AHEAD |= {name: HC for name in ("fc1", "gelu", "h_hi", "h_lo")}
        COUNT |= {name: TILES for name in ("xtr", "x_in", "otr", "y_ready")}
        AHEAD |= {name: 0 for name in ("xtr", "x_in", "otr", "y_ready")}
        COUNT["exp_loaded"], AHEAD["exp_loaded"] = PHASES, 1
        S = {name: sem(name) for name in COUNT}
        x_loaded = sem("x_loaded")
        x_ordered = sem("x_ordered")
        y_stored = sem("y_stored")

        def when(eng, it, name, n):
            eng.wait_ge(S[name], it * COUNT[name] + (n + 1 + AHEAD[name] + CREDIT))

        def stream(n, which):
            layer, t = visit(n)
            return x_tok[:, t, :] if layer else (x_new, x_mid)[which][:, t % GROUP, :]

        def run(eng, slot):
            for s in range(-2 * GROUP, FIRST):
                slot(0, s, lambda n: n >= -GROUP)
            with eng.Fori(0, IMAGES) as it:
                for s in range(FIRST, LAST):
                    slot(it, s, lambda n: True)
            for s in range(LAST, STEPS + GROUP + 8):
                slot(IMAGES - 1, s, lambda n: n < STEPS + GROUP)

        def v_places(n, par, w, part):
            src = ps_v[w * WIN:(w + 1) * WIN, 0:C].rearrange("p (g a d) -> p g a d", a=2, d=HD)[:, :, par]
            return src, v_blk[par * 64:par * 64 + 64, n % 2, part, :, par, w, 0:HD]

        block = ctx.enter_context(nc.Block())
        A, B = slice(CB, C), slice(0, CB)

        @block.sync
        def _(sp):
            sp.sem_inc(y_stored, 16)
            span = 2 * WS - 1

            def twice(v, a, n):
                return bass.AP(tensor=v.tensor, offset=v.offset + a, ap=[[0, 2], [n, CB], [1, n]])

            def column(v, a):
                return v[a:a + 128].rearrange("(c a) -> c a", a=1)

            for l, L in enumerate(layers):
                for i, name in enumerate(("g1", "b1", "g2", "b2")):
                    sp.dma_start(cols[:, l, i, 0:1], column(L[name], CB)).then_inc(norm_in[l], 16)
                    sp.dma_start(cols[:, l, i, 1:2], twice(L[name], 0, 1)).then_inc(norm_in[l], 16)
                for k, (name, n) in enumerate((("wqkv", 3 * C), ("wproj", C), ("wfc1", HID), ("wfc2", 0))):
                    j = 4 * l + k
                    if j >= 2:
                        sp.wait_ge(made, j)
                    if n:
                        sp.dma_start(stage[:, j % 2, 0, 0:n], L[name][A, :]).then_inc(w_in[j], 16)
                        sp.dma_start(stage[:, j % 2, 1, 0:n], twice(L[name], 0, n)).then_inc(w_in[j], 16)
                    else:
                        sp.dma_start(stage[:, j % 2].rearrange("p a n -> p (a n)")[:, 0:HC * C]
                                     .rearrange("p (m c) -> p m c", m=HC),
                                     L[name].rearrange("(m p) c -> p m c", p=128)).then_inc(w_in[j], 16)
                    if k == 0:
                        for i, (bias, m) in enumerate((("bqkv", 3 * C), ("bproj", C), ("bfc2", C))):
                            o = (0, 3 * C, 4 * C)[i]
                            sp.dma_start(row[:, o:o + m], L[bias].rearrange("(a c) -> a c", a=1)).then_inc(w_in[j], 16)
                        sp.dma_start(vcol[:, 0:1], column(L["bqkv"], 2 * C + CB)).then_inc(w_in[j], 16)
                        sp.dma_start(vcol[:, 1:2], twice(L["bqkv"], 2 * C, 1)).then_inc(w_in[j], 16)
                    if k == 2:
                        sp.dma_start(b_fc1[l][:, :], L["bfc1"].rearrange("(m p) -> p m", p=128),
                                     allow_slow_non_contiguous=True).then_inc(w_in[j], 16)
                    if j == 0:
                        sp.dma_start(ident[:, :], ident_in).then_inc(const_in[0], 16)
                        sp.dma_start(x_img[:, :, :], x[0].rearrange("(k p) h w -> p k (h w)", k=2)).then_inc(x_loaded, 16)
                    if j == 1:
                        for w in range(2):
                            for qr in range(WS):
                                src = bass.AP(tensor=rel_bias.tensor, offset=rel_bias.offset + qr * span * HEADS,
                                              ap=[[HEADS, WS], [span * HEADS, WS], [1, WS * HEADS]])
                                p0 = w * WIN + qr * WS
                                sp.dma_start(rel[p0:p0 + WS, :, :].rearrange("p (a b) h -> p a (b h)", a=WS), src)\
                                    .then_inc(const_in[2], 16)
                        sp.dma_start(q_mask[:, :], q_mask_in).then_inc(const_in[1], 16)
                        sp.dma_start(k_mask[:, :, :], k_mask_in).then_inc(const_in[1], 16)

            def next_image(it):
                sp.wait_ge(x_ordered, 2 * it + 2)
                following = (it + 1) % IMAGES
                sp.dma_start(x_img[:, :, :], x[following if isinstance(it, int) else sp.snap(following)]
                             .rearrange("(k p) h w -> p k (h w)", k=2)).then_inc(x_loaded, 16)

            def store(image):
                sp.dma_start(out[image].rearrange("(k p) h w -> p k (h w)", k=2), y_img[:, :, :])\
                    .then_inc(y_stored, 16)

            next_image(0)
            with sp.Fori(1, IMAGES) as it:
                next_image(it)
                when(sp, it, "y_ready", GROUP - 1)
                store(sp.snap(it - 1))
            when(sp, IMAGES - 1, "y_ready", TILES + GROUP - 1)
            store(IMAGES - 1)
            sp.wait_ge(y_stored, 16 * (IMAGES + 1))
            sp.wait_ge(x_loaded, 16 * (IMAGES + 1))

        W_DMAS = [7, 2, 3, 1]

        @block.tensor
        def _(pe):
            mm = nc.tensor.matmul
            for name in ("tr1", "qk_mm", "v_mm", "tqk", "s_mm", "shift", "tp", "pv", "to", "pr", "tr2", "fc1", "fc2",
                         "xtr", "otr"):
                pe.sem_inc(S[name], CREDIT)

            for l in range(LAYERS):
                sA1, sB1 = cols[:, l, 1, 0:1], cols[0:CB, l, 1, 1:2]
                sA2, sB2 = cols[:, l, 3, 0:1], cols[0:CB, l, 3, 1:2]
                pe.wait_ge(norm_in[l], 16 * 8)
                pe.wait_ge(w_in[4 * l], 16 * W_DMAS[0])
                pe.wait_ge(made, 1 + 4 * l)
                mm(ps_qk[0:1, 0:2 * C], sA1, stage[:, 0, 0, 0:2 * C], start=True, stop=False)
                mm(ps_qk[0:1, 0:2 * C], sB1, stage[0:CB, 0, 1, 0:2 * C], start=False, stop=True)
                for j, cs in enumerate((slice(2 * C + CB, 3 * C), slice(2 * C, 2 * C + CB))):
                    m = cs.stop - cs.start
                    mm(ps_v[0:m, j:j + 1], stage[:, 0, 0, cs], sA1, start=True, stop=False)
                    last = mm(ps_v[0:m, j:j + 1], stage[0:CB, 0, 1, cs], sB1, start=False, stop=True)
                last.then_inc(folded, 1)
                pe.wait_ge(w_in[4 * l + 1], 16 * W_DMAS[1])
                pe.wait_ge(made, 2 + 4 * l)
                mm(ps_o[0:1, 0:C], vcol[:, 0:1], stage[:, 1, 0, 0:C], start=True, stop=False)
                mm(ps_o[0:1, 0:C], vcol[0:CB, 1:2], stage[0:CB, 1, 1, 0:C], start=False, stop=True).then_inc(folded, 1)
                pe.wait_ge(w_in[4 * l + 2], 16 * W_DMAS[2])
                for m in range(HC):
                    cs = slice(m * 128, (m + 1) * 128)
                    mm(ps_s[:, 0, m:m + 1], stage[:, 0, 0, cs], sA2, start=True, stop=False)
                    last = mm(ps_s[:, 0, m:m + 1], stage[0:CB, 0, 1, cs], sB2, start=False, stop=True)
                last.then_inc(folded, 1)
                pe.wait_ge(made, 3 + 4 * l)
                mm(ps_t[:, 0, 0:2 * C], ones_row[:, :], rowsum[:, :], start=True, stop=True).then_inc(folded, 1)
            pe.wait_ge(made, 1 + 4 * LAYERS)
            pe.wait_ge(tables, 1)


            def slot(it, s, live):
                def ge(name, n):
                    when(pe, it, name, n)

                def take_tr(reader, n):
                    ge(*tr_reader)
                    tr_reader[:] = [reader, n]

                def contract(dst, w, lhs_tile, n0, n1, last_block=1):
                    for i, (blk, part) in enumerate(((0, 0), (2, 0), (0, 1), (1, 2), (last_block, 3))):
                        last = mm(dst, lhs_tile(blk), w[:, part, n0:n1], start=(i == 0), stop=(i == 4))
                    return last

                def transpose3(dst16, src):
                    nc.tensor.transpose(dst16[:, 0:TOK], src[:, 0, A], ident16[:, :])
                    for part in range(2):
                        nc.tensor.transpose(dst16[part * CB:(part + 1) * CB, TOK:2 * TOK], src[:, part, B], ident16[:, :])
                    return nc.tensor.transpose(dst16[:, 2 * TOK:3 * TOK], src[:, 1, A], ident16[:, :])

                def x_transpose(n):
                    layer, t = visit(n)
                    take_tr("x_in", visit_in_layer(n))
                    if t % GROUP == 0:
                        pe.wait_ge(x_ordered, 2 * (it + (n + GROUP) // STEPS) + t // GROUP + 1)
                    for k in range(2):
                        last = nc.tensor.transpose(ps_tr[:, k * H2:(k + 1) * H2], x_win[:, k, t * TOK:(t + 1) * TOK],
                                                   ident[0:H2, 0:H2])
                    last.then_inc(S["xtr"], 1)

                def norm1_transpose(n):
                    take_tr("xt_done", n)
                    if s == FIRST:
                        ge("y_ready", -1)
                    ge("lo1", n)
                    transpose3(ps_tr16, xs[:, 0, n % 2]).then_inc(S["tr1"], 1)

                def qk_product(n):
                    layer, t = visit(n)
                    ge("resid1", n - 4)
                    ge("xt_done", n)
                    contract(ps_qk[:, 0:2 * C], w_qkv[layer], lambda b: xt[:, n % 2, b, :], 0, 2 * C,
                             last_block=3).then_inc(S["qk_mm"], 1)

                def v_product(n):
                    layer, t = visit(n)
                    if in_v is not None:
                        ge("resid2", in_v)
                    else:
                        ge("v_lo", n - 1)
                    contract(ps_v[:, 0:C], w_qkv[layer], lambda b: xt[:, n % 2, b, :], 2 * C, 3 * C)\
                        .then_inc(S["v_mm"], 1)

                def qk_transpose(n):
                    ge("p_lo", n - 2)
                    ge("qk_lo", n)
                    ge("mask_set", n)
                    for qk_half in range(2):
                        for g in range(PAIRS):
                            h = qk_half * HEADS + 2 * g
                            last = nc.tensor.transpose(ps_t16[qk_half][:, g * TOK:(g + 1) * TOK],
                                                       qk[:, n % 2, h:h + 2].rearrange("p h s d -> p (h s d)"),
                                                       ident16[:, :])
                    last.then_inc(S["tqk"], 1)

                def scores(n):
                    layer, t = visit(n)
                    p, place = mlp_phase(n)
                    if place == 0 and p >= -1:
                        ge("gelu", p * HC + HC - 1)
                    ge("exp_done", n - 1)
                    ge("q_evac", n)
                    ge("k_evac", n)
                    if layer == 0:
                        for par in range(2):
                            mm(ps_s[:, par, 0:PAIRS * WIN], pair_ident[:, :], bias_tab[:, par, :, :],
                               start=True, stop=False, skip_group_check=True)
                    else:
                        pe.nop(nofuse=True)
                    for g in range(PAIRS):
                        for w in range(2):
                            for par in range(2):
                                rows = slice(par * 64, par * 64 + 64)
                                tok = slice(w * WIN, (w + 1) * WIN)
                                last = mm(ps_s[w * WIN:(w + 1) * WIN, par, g * WIN:(g + 1) * WIN],
                                          qt[rows, n % 2, g, tok], kt[rows, n % 2, g, tok],
                                          start=(layer == 1 and g == 0), stop=False, skip_group_check=True)
                    last.then_inc(S["s_mm"], 1)

                def shift_scores(n):
                    ge("max_done", n)
                    for par in range(2):
                        last = mm(ps_s[:, par, 0:PAIRS * WIN].rearrange("p (g k) -> p g k", g=PAIRS), neg_ident[:, :],
                                  smax[:, n % 2, par, :].unsqueeze(2).broadcast_to([128, PAIRS, WIN]),
                                  start=False, stop=True, skip_group_check=True)
                    last.then_inc(S["shift"], 1)

                def p_transpose(n):
                    if not live(n + 1):
                        ge("p_lo", n - 1)
                    ge("exp_done", n)
                    for g in range(PAIRS):
                        last = nc.tensor.transpose(ps_t[:, g // 3, (g % 3) * TOK:(g % 3 + 1) * TOK],
                                                   p_tok[:, n % 2, g].rearrange("p a k -> p (a k)"), ident[:, :])
                    last.then_inc(S["tp"], 1)

                def pv_product(n):
                    ge("ot_done", n - 1)
                    ge("v_lo", n)
                    ge("p_lo", n)
                    for g in range(PAIRS):
                        for i, (ps, vs) in enumerate(((0, 0), (0, 1), (1, 0))):
                            last = mm(ps_o[:, g * 4 * VW:(g + 1) * 4 * VW], pt[:, n % 2, ps, g, :],
                                      v_blk[:, n % 2, vs, g].rearrange("p a w d -> p (a w d)"),
                                      start=(i == 0), stop=(i == 2))
                    last.then_inc(S["pv"], 1)

                def o_transpose(n):
                    q, at = mlp_phase(s - 1)
                    if q >= -1 and at == 1:
                        ge("resid2", q * GROUP + 1)
                    ge("o_lo", n)
                    transpose3(ps_o16, os[:, n % 2]).then_inc(S["to"], 1)

                def projection(n):
                    layer, t = visit(n)
                    if live(n + 3):
                        ge("qk_lo", n + 3)
                    else:
                        ge("resid1", n - 1)
                    ge("ot_done", n)
                    contract(ps_qk[:, 0:C], w_proj[layer], lambda b: ot[:, n % 2, b, :], 0, C)\
                        .then_inc(S["pr"], 1)

                def norm2_transpose(n):
                    take_tr("ht_done", n)
                    ge("lo2", n)
                    transpose3(ps_tr16, xs[:, 1, n % 2]).then_inc(S["tr2"], 1)

                def hidden(m):
                    layer, _ = visit(p * GROUP)
                    u = p * HC + m
                    if m == 0:
                        ge("ht_done", p * GROUP + GROUP - 1)
                        ge("exp_done", min(s - 1, end))
                    if m >= 2:
                        ge("gelu", u - 2)
                    for i, (part, blk) in enumerate(((0, 0), (0, 2), (1, 0), (2, 1), (3, 1))):
                        last = mm(ps_s[:, u % 2, :], w_fc1[layer][:, part, m * 128:(m + 1) * 128],
                                  ht[:, p % 2, blk, :], start=(i == 0), stop=(i == 4))
                    last.then_inc(S["fc1"], 1)

                def mlp_out(n, bank):
                    layer, t = visit(n)
                    tok = slice((t % GROUP) * TOK, (t % GROUP + 1) * TOK)
                    if n % GROUP == 0:
                        ge("h_lo", p * HC + HC - 1)
                    for m in range(HC):
                        for i, (hs, ws) in enumerate(((0, 0), (0, 1), (1, 0))):
                            last = mm(bank[:, 0:C], hid16[:, hs, m, tok], w_fc2[layer][:, ws, m, :],
                                      start=(m == 0 and i == 0), stop=(m == HC - 1 and i == 2))
                    last.then_inc(S["fc2"], 1)

                def y_transpose(n):
                    layer, t = visit(n)
                    take_tr("y_ready", visit_in_layer(n))
                    ge("resid2", n)
                    for k in range(2):
                        last = nc.tensor.transpose(ps_tr[0:H2, k * TOK:(k + 1) * TOK], x_tok[:, t, k * H2:(k + 1) * H2],
                                                   ident[:, :])
                    last.then_inc(S["otr"], 1)

                p, place = mlp_phase(s)
                end = STEPS + GROUP - 1
                mlp = p >= -1
                hid_slot, out_slot = mlp and place == 0, mlp and place > 0
                in_v = p * GROUP + (0, 0, 2, 3)[place] if out_slot else None
                last_block = out_slot and visit(p * GROUP)[0] == 1
                x_due = live(s + 4) and visit(s + 4)[0] == 0
                if live(s):
                    qk_product(s)
                if live(s + 1):
                    norm1_transpose(s + 1)
                if hid_slot:
                    if live(s - 3):
                        o_transpose(s - 3)
                    hidden(0)
                    hidden(1)
                if out_slot:
                    ge("v_lo", min(s - 1, end))
                    if s - 1 > end:
                        ge("resid2", in_v - 1)
                    mlp_out(in_v, ps_v)
                    if last_block and place == 2:
                        y_transpose(p * GROUP + 1)
                if live(s - 3) and not hid_slot:
                    o_transpose(s - 3)
                if live(s):
                    qk_transpose(s)
                if live(s - 2) and not hid_slot:
                    pv_product(s - 2)
                if hid_slot:
                    for m in range(2, HC):
                        if m == 4 and live(s - 4):
                            norm2_transpose(s - 4)
                        hidden(m)
                if x_due:
                    x_transpose(s + 4)
                if live(s - 2) and hid_slot:
                    pv_product(s - 2)
                if live(s - 3):
                    projection(s - 3)
                if live(s):
                    scores(s)
                    v_product(s)
                if not hid_slot:
                    if live(s - 4):
                        norm2_transpose(s - 4)
                if live(s - 1):
                    p_transpose(s - 1)
                if out_slot and place == 1:
                    ge("o_evac", min(s - 2, end))
                    if s - 2 > end:
                        ge("ot_done", end)
                    mlp_out(p * GROUP + 1, ps_o)
                if last_block:
                    y_transpose(p * GROUP + place - (place == 1))
                if live(s):
                    shift_scores(s)

            tr_reader = ["x_in", -1]
            run(pe, slot)

        @block.scalar
        def _(act):
            copy = nc.scalar.activation
            for name in ("x_in", "xt_done", "qk_hi", "v_hi", "k_evac", "exp_done", "p_hi", "o_evac",
                         "hi2", "ht_done", "gelu", "y_ready", "exp_loaded"):
                act.sem_inc(S[name], CREDIT)
            act.wait_ge(made, 1 + 4 * LAYERS)

            def slot(it, s, live):
                def ge(name, n):
                    when(act, it, name, n)

                def x_evac(n):
                    ge("xtr", visit_in_layer(n))
                    copy(stream(n, 0), ps_tr[:, 0:C], ACT.Copy).then_inc(S["x_in"], 1)

                def norm2_hi(n):
                    ge("ln2", n)
                    ge("tr2", n - 2)
                    copy(xs[:, 1, n % 2, 0, :], xn[:, 1, n % 2, :], ACT.Copy).then_inc(S["hi2"], 1)

                def xt_evac(n):
                    ge("tr1", n)
                    copy(xt[:, n % 2, 0:3].rearrange("p b t -> p (b t)"), ps_tr16[:, 0:3 * TOK], ACT.Copy)
                    copy(xt[0:CB, n % 2, 3, :], ps_tr16[0:CB, TOK:2 * TOK], ACT.Copy)\
                        .then_inc(S["xt_done"], 1)

                def ht_evac(n):
                    ge("tr2", n)
                    copy(ht[:, n // GROUP % 2, :, (n % GROUP) * TOK:(n % GROUP + 1) * TOK],
                         ps_tr16[:, 0:3 * TOK].rearrange("p (b t) -> p b t", b=3), ACT.Copy).then_inc(S["ht_done"], 1)

                def qk_hi(n):
                    ge("qk_mm", n)
                    for i, places in enumerate((slice(0, 2), slice(0, 3, 2))):
                        src = ps_qk[:, i * C:(i + 1) * C].rearrange("p (h d) -> p h d", d=HD).unsqueeze(2)
                        last = copy(qk[:, n % 2, i * HEADS:(i + 1) * HEADS, places, :],
                                    src.broadcast_to([128, HEADS, 2, HD]), ACT.Copy, scale=UNSCALE)
                    last.then_inc(S["qk_hi"], 1)

                def v_hi(n):
                    ge("v_mm", n)
                    for par in range(2):
                        for w in range(2):
                            src, dst = v_places(n, par, w, 0)
                            last = copy(dst, src, ACT.Copy, scale=UNSCALE)
                    last.then_inc(S["v_hi"], 1)

                def k_evac(n):
                    ge("tqk", n)
                    copy(kt[:, n % 2].rearrange("p g t -> p (g t)"), ps_t16[1][:, 0:PAIRS * TOK], ACT.Copy)\
                        .then_inc(S["k_evac"], 1)

                def exp(n):
                    ge("shift", n)
                    nc.scalar.activation(p_tok[:, n % 2].rearrange("p g a k -> p a g k"),
                                         ps_s[:, :, 0:PAIRS * WIN].rearrange("p a (g k) -> p a g k", g=PAIRS),
                                         ACT.Exp).then_inc(S["exp_done"], 1)

                def p_hi(n):
                    ge("tp", n)
                    copy(pt[:, n % 2, 0].rearrange("p (b g) t -> p b (g t)", b=2), ps_t[:, :, 0:3 * TOK], ACT.Copy)\
                        .then_inc(S["p_hi"], 1)

                def o_evac(n):
                    ge("pv", n)
                    for w in range(2):
                        rows = slice(w * WIN, (w + 1) * WIN)
                        src = ps_o[rows, 0:4 * PAIRS * VW].rearrange("p (h w d) -> p h w d", w=2, d=VW)[:, :, w]
                        last = copy(o_raw[rows, n % 2], src, ACT.Copy)
                    last.then_inc(S["o_evac"], 1)

                def gelu(m):
                    layer, _ = visit(p * GROUP)
                    u = p * HC + m
                    ge("fc1", u)
                    ge("h_lo", u - 2)
                    nc.scalar.activation(hid[:, u % 2, :], ps_s[:, u % 2, :], ACT.Gelu, bias=b_fc1[layer][:, m:m + 1],
                                         scale=UNSCALE).then_inc(S["gelu"], 1)

                def load_exp():
                    ge("exp_loaded", p - 1)
                    nc.scalar.activation(spare[:, :], half[0:1, :], ACT.Exp).then_inc(S["exp_loaded"], 1)

                def y_evac(n):
                    layer, t = visit(n)
                    ge("otr", visit_in_layer(n))
                    if t == 0:
                        act.wait_ge(y_stored, it * 16 + 16)
                    tile = ps_tr[0:H2, 0:2 * TOK].rearrange("p (k t) -> p k t", k=2)
                    for win, img in box_pairs(t, tile, y_img[:, :, :]):
                        last = copy(img, win, ACT.Copy)
                    last.then_inc(S["y_ready"], 1)

                p, place = mlp_phase(s)
                mlp = p >= -1
                hid_slot = mlp and place == 0
                last_block = mlp and place and visit(p * GROUP)[0] == 1
                x_due = live(s + 4) and visit(s + 4)[0] == 0
                if live(s):
                    qk_hi(s)
                if live(s + 1):
                    xt_evac(s + 1)
                if hid_slot:
                    gelu(0)
                if live(s - 4) and hid_slot:
                    norm2_hi(s - 4)
                if last_block and place == 2:
                    y_evac(p * GROUP + 1)
                if hid_slot:
                    gelu(1)
                if live(s):
                    k_evac(s)
                if hid_slot:
                    gelu(2)
                if live(s - 2) and not hid_slot:
                    o_evac(s - 2)
                if live(s - 4) and not hid_slot:
                    norm2_hi(s - 4)
                if hid_slot:
                    gelu(3)
                    if live(s - 4):
                        ht_evac(s - 4)
                    gelu(4)
                    gelu(5)
                if x_due:
                    x_evac(s + 4)
                if hid_slot:
                    if live(s - 2):
                        o_evac(s - 2)
                    load_exp()
                if live(s):
                    v_hi(s)
                if not hid_slot:
                    if live(s - 4):
                        ht_evac(s - 4)
                if live(s - 1):
                    p_hi(s - 1)
                if last_block:
                    y_evac(p * GROUP + place - (place == 1))
                if live(s):
                    exp(s)

            run(act, slot)

        @block.vector
        def _(dve):
            v = nc.vector
            for name in ("bn1a", "bn1", "qk_lo", "v_lo", "q_evac", "max_done", "p_lo", "inv_done",
                         "ot_done", "resid1", "bn2a", "bn2", "lo2", "h_lo", "resid2"):
                dve.sem_inc(S[name], CREDIT)

            steps = [0]

            def link(ins):
                steps[0] += 1
                ins.then_inc(dve_chain, 1)
                dve.wait_ge(dve_chain, steps[0])

            v.memset(xt[CB:128, :, 3, :], 1.0)
            v.memset(ones_row[:, :], 1.0)
            v.memset(half[:, :], -0.5)
            v.memset(x_tok[:, :, :].rearrange("p t c -> p (t c)"), 0.0)
            v.memset(qk[:, :].rearrange("p r h s d -> p (r h s d)"), 0.0)
            link(v.memset(v_blk[:, :].rearrange("p r s g a w d -> p (r s g a w d)"), 0.0))
            for par in range(2):
                for r in range(2):
                    v.memset(v_blk[par * 64:par * 64 + 64, r, 0, :, par, :, HD:VW], 1.0)
            dve.wait_ge(const_in[0], 16)
            for w in range(2):
                v.tensor_tensor(pair_ident[:, w * WIN:(w + 1) * WIN], ident[:, 0:WIN], ident[:, WIN:TOK], ALU.add)
            link(v.tensor_copy(ident16[:, :], ident[:, :]))
            v.tensor_scalar(neg_ident[:, :], ident[:, :], -1.0, None, ALU.mult).then_inc(made, 1)

            def split(hi, lo, src):
                link(v.tensor_copy(hi, src))
                link(v.tensor_tensor(lo, src, hi, ALU.subtract))

            def make_weight(w, place, n, gain, q_cols=0):
                for ab in range(2):
                    for c0, c1, s in ((0, q_cols, WSCALE * QSCALE), (q_cols, n, WSCALE)):
                        if c1 > c0:
                            src, dst = stage[:, place, ab, c0:c1], scaled[:, ab, c0:c1]
                            if gain is None:
                                link(v.tensor_scalar(dst, src, s, None, ALU.mult))
                            else:
                                link(v.tensor_scalar(dst, src, gain[:, ab:ab + 1], s, ALU.mult, ALU.mult))
                    split(w[:, 2 * ab, 0:n], w[:, 2 * ab + 1, 0:n], scaled[:, ab, 0:n])

            for l in range(LAYERS):
                dve.wait_ge(norm_in[l], 16 * 8)
                dve.wait_ge(w_in[4 * l], 16 * W_DMAS[0])
                make_weight(w_qkv[l], 0, 3 * C, cols[:, l, 0, :], q_cols=C)
                dve.wait_ge(folded, 4 * l + 1)
                link(v.tensor_tensor(row[:, 0:2 * C], row[:, 0:2 * C], ps_qk[0:1, 0:2 * C], ALU.add))
                link(v.tensor_scalar(row[:, 0:C], row[:, 0:C], WSCALE * QSCALE, None, ALU.mult))
                link(v.tensor_scalar(row[:, C:2 * C], row[:, C:2 * C], WSCALE, None, ALU.mult))
                link(v.memset(w_qkv[l][CB:128, 3, 0:2 * C], 0.0))
                link(v.tensor_copy(row16[:, :], row[:, 0:2 * C]))
                link(v.tensor_copy(w_qkv[l][64:65, 3, 0:2 * C], row16[:, :]))
                link(v.tensor_tensor(w_qkv[l][96:97, 3, 0:2 * C], row[:, 0:2 * C], row16[:, :], ALU.subtract))
                link(v.tensor_tensor(vcol[:, 0:1], vcol[:, 0:1], ps_v[:, 0:1], ALU.add))
                v.tensor_tensor(vcol[0:CB, 1:2], vcol[0:CB, 1:2], ps_v[0:CB, 1:2], ALU.add).then_inc(made, 1)
                dve.wait_ge(w_in[4 * l + 1], 16 * W_DMAS[1])
                make_weight(w_proj[l], 1, C, None)
                dve.wait_ge(folded, 4 * l + 2)
                link(v.tensor_tensor(rowsum[:, 0:C], row[:, 3 * C:4 * C], ps_o[0:1, 0:C], ALU.add))
                v.tensor_copy(rowsum[:, C:2 * C], row[:, 4 * C:5 * C]).then_inc(made, 1)
                dve.wait_ge(w_in[4 * l + 2], 16 * W_DMAS[2])
                make_weight(w_fc1[l], 0, HID, cols[:, l, 2, :])
                dve.wait_ge(folded, 4 * l + 3)
                v.tensor_tensor(b_fc1[l][:, :], b_fc1[l][:, :], ps_s[:, 0, 0:HC], ALU.add).then_inc(made, 1)
                dve.wait_ge(w_in[4 * l + 3], 16 * W_DMAS[3])
                flat = stage[:, 1].rearrange("p a n -> p (a n)")[:, 0:HC * C]
                flat2 = scaled[:, :, :].rearrange("p a n -> p (a n)")[:, 0:HC * C]
                link(v.tensor_scalar(flat2, flat, WSCALE, None, ALU.mult))
                split(w_fc2[l][:, 0].rearrange("p m c -> p (m c)"), w_fc2[l][:, 1].rearrange("p m c -> p (m c)"), flat2)
                dve.wait_ge(folded, 4 * l + 4)
                link(v.tensor_copy(b_proj[l][:, :], ps_t[:, 0, 0:C]))
                v.tensor_copy(b_fc2[l][:, :], ps_t[:, 0, C:2 * C]).then_inc(made, 1)
            def slot(it, s, live):
                def ge(name, n):
                    when(dve, it, name, n)

                def statistics(n, which):
                    a = "12"[which]
                    layer, _ = visit(n)
                    if which == 1:
                        ge("resid1", n)
                    elif layer == 0:
                        ge("x_in", visit_in_layer(n))
                    elif n >= STEPS - GROUP or s >= FIRST:
                        ge("resid2", n - 3 * GROUP)
                    v.bn_stats(bn6[:, which, n % 2, :], stream(n, which)).then_inc(S[f"bn{a}a"], 1)

                def mean_variance(n, which):
                    a = "12"[which]
                    ge(f"bn{a}a", n)
                    ge("ln" + a, n - 2)
                    dve.nop(nofuse=True)
                    v.bn_aggr(mv[:, which, n % 2, :], bn6[:, which, n % 2, :]).then_inc(S["bn" + a], 1)

                def norm_lo(n):
                    ge("hi2", n)
                    v.tensor_tensor(xs[:, 1, n % 2, 1, :], xn[:, 1, n % 2, :], xs[:, 1, n % 2, 0, :],
                                    ALU.subtract).then_inc(S["lo2"], 1)

                def qk_lo(n):
                    ge("qk_hi", n)
                    for i, place in enumerate((2, 1)):
                        heads = slice(i * HEADS, (i + 1) * HEADS)
                        last = v.scalar_tensor_tensor(
                            out=qk[:, n % 2, heads, place, :],
                            in0=ps_qk[:, i * C:(i + 1) * C].rearrange("p (h d) -> p h d", d=HD), scalar=UNSCALE,
                            in1=qk[:, n % 2, heads, 0, :], op0=ALU.mult, op1=ALU.subtract)
                    last.then_inc(S["qk_lo"], 1)

                def v_lo(n):
                    ge("v_hi", n)
                    for par in range(2):
                        for w in range(2):
                            src, dst = v_places(n, par, w, 1)
                            last = v.scalar_tensor_tensor(out=dst, in0=src, scalar=UNSCALE,
                                                          in1=v_places(n, par, w, 0)[1],
                                                          op0=ALU.mult, op1=ALU.subtract)
                    last.then_inc(S["v_lo"], 1)

                def q_evac(n):
                    ge("tqk", n)
                    v.tensor_copy(qt[:, n % 2].rearrange("p g t -> p (g t)"), ps_t16[0][:, 0:PAIRS * TOK])\
                        .then_inc(S["q_evac"], 1)

                def row_max(n):
                    ge("s_mm", n)
                    v.tensor_reduce(smax[:, n % 2], ps_s[:, :, 0:PAIRS * WIN].rearrange("p a (g k) -> p a g k", g=PAIRS),
                                    AX.X, ALU.max).then_inc(S["max_done"], 1)

                def p_lo(n):
                    ge("p_hi", n)
                    v.tensor_tensor(pt[:, n % 2, 1].rearrange("p (b g) t -> p b (g t)", b=2), ps_t[:, :, 0:3 * TOK],
                                    pt[:, n % 2, 0].rearrange("p (b g) t -> p b (g t)", b=2), ALU.subtract)\
                        .then_inc(S["p_lo"], 1)

                def inverse_sums(n):
                    ge("o_evac", n)
                    v.reciprocal(o_inv[:, n % 2, :], o_raw[:, n % 2, :, HD]).then_inc(S["inv_done"], 1)

                def ot_evac(n):
                    ge("to", n)
                    v.tensor_copy(ot[:, n % 2].rearrange("p b t -> p (b t)"), ps_o16[:, 0:3 * TOK])\
                        .then_inc(S["ot_done"], 1)

                def residual(n, src, out, old, product, bias, done):
                    ge(product, n)
                    ge(bias, n)
                    v.scalar_tensor_tensor(out=out, in0=src, scalar=UNSCALE, in1=old,
                                           op0=ALU.mult, op1=ALU.add).then_inc(S[done], 1)

                def attention_residual(n):
                    residual(n, ps_qk[:, 0:C], stream(n, 1), stream(n, 0), "pr", "bias1", "resid1")

                def mlp_residual(n, bank):
                    residual(n, bank[:, 0:C], x_tok[:, visit(n)[1], :], stream(n, 1), "fc2", "bias2", "resid2")

                def hidden_lo(m):
                    u = p * HC + m
                    ge("gelu", u)
                    ge("h_hi", u)
                    v.tensor_tensor(hid16[:, 1, m, :], hid[:, u % 2, :], hid16[:, 0, m, :], ALU.subtract)\
                        .then_inc(S["h_lo"], 1)

                p, place = mlp_phase(s)
                mlp = p >= -1
                hid_slot = mlp and place == 0
                if live(s):
                    qk_lo(s)
                if mlp and place:
                    mlp_residual(p * GROUP + (0, 0, 2, 3)[place], ps_v)
                if live(s - 3):
                    ot_evac(s - 3)
                if live(s):
                    q_evac(s)
                if mlp and place == 1 and live(s + 2):
                    statistics(s + 2, 0)
                    mean_variance(s + 2, 0)
                if live(s - 4) and hid_slot:
                    norm_lo(s - 4)
                if hid_slot:
                    hidden_lo(0)
                    hidden_lo(1)
                    hidden_lo(2)
                if live(s - 2) and not hid_slot:
                    inverse_sums(s - 2)
                if hid_slot:
                    hidden_lo(3)
                    hidden_lo(4)
                if live(s - 3):
                    attention_residual(s - 3)
                if live(s - 4) and not hid_slot:
                    norm_lo(s - 4)
                if live(s - 2) and hid_slot:
                    inverse_sums(s - 2)
                if live(s):
                    row_max(s)
                if hid_slot:
                    hidden_lo(5)
                if live(s):
                    v_lo(s)
                if live(s - 1):
                    p_lo(s - 1)
                if mlp and place == 1:
                    mlp_residual(p * GROUP + 1, ps_o)
                norms = [(n, which) for n, which in ((s - 3, 1), (s + 3, 0))
                         if live(n) and not (hid_slot and which == 0)]
                for n, which in norms:
                    statistics(n, which)
                for n, which in norms:
                    mean_variance(n, which)

            run(dve, slot)

        @block.gpsimd
        def _(pool):
            g_ = nc.gpsimd
            for name in ("mask_set", "ln1a", "ln1b", "ln1", "bias1", "hi1", "lo1", "o_norm", "o_hi", "o_lo", "ln2a", "ln2b", "ln2", "bias2", "h_hi"):
                pool.sem_inc(S[name], CREDIT)

            def order_tile(t):
                for win, img in box_pairs(t, x_win[:, :, t * TOK:(t + 1) * TOK], x_img[:, :, :]):
                    last = g_.tensor_scalar(win, img, 1.0, 0.0, ALU.mult, ALU.add)
                if t % GROUP == GROUP - 1:
                    last.then_inc(x_ordered, 1)

            ORDERED = {4: (0, 1), 5: (2, 3), 12: (4, 5, 6), 13: (7,)}

            def order_tiles(it, s):
                if ORDERED[s][0] % GROUP == 0:
                    when(pool, it, "xtr", ORDERED[s][0] + GROUP - 1)
                if s == FIRST:
                    pool.wait_ge(x_loaded, it * 16 + 32)
                pool.nop(nofuse=True)
                for t in ORDERED[s]:
                    order_tile(t)

            pool.wait_ge(x_loaded, 16)
            for t in range(TILES):
                order_tile(t)

            steps = [0]

            def link(ins):
                steps[0] += 1
                ins.then_inc(pool_chain, 1)
                pool.wait_ge(pool_chain, steps[0])

            pool.wait_ge(const_in[2], 16 * 2 * WS)
            for key in range(WIN):
                last = g_.tensor_scalar(rel_t[:, :, :, key], rel[:, WIN - 1 - key, :].rearrange("p (g a) -> p a g", a=2),
                                        1.0, 0.0, ALU.mult, ALU.add)
            link(last)
            low = slice(WIN, TOK)
            link(g_.tensor_scalar(bias_tab[:, :], rel_t[:, :], 1.0, 0.0, ALU.mult, ALU.add))
            link(g_.tensor_tensor(bias_tab[low, :], rel_t[low, :], bias_tab[low, :], ALU.subtract))
            pool.wait_ge(const_in[1], 2 * 16)
            pool.wait_ge(made, 1)
            for r in range(2):
                last = g_.tensor_scalar(qk[:, r, 0:HEADS, 3, 0:REGIONS],
                                        q_mask[:, :].unsqueeze(1).broadcast_to([128, HEADS, REGIONS]),
                                        1.0, 0.0, ALU.mult, ALU.add)
            last.then_inc(tables, 1)
            pool.wait_ge(made, 1 + 4 * LAYERS)

            def slot(it, s, live):
                def ge(name, n):
                    when(pool, it, name, n)

                def set_mask(n):
                    layer, t = visit(n)
                    kind = 2 * (t // 2 == 3) + t % 2 if layer == 0 else KINDS
                    ge("tqk", n - 2)
                    pool.nop(nofuse=True)
                    g_.tensor_scalar(qk[:, n % 2, HEADS:2 * HEADS, 3, 0:REGIONS],
                                     k_mask[:, kind, :].unsqueeze(1).broadcast_to([128, HEADS, REGIONS]),
                                     1.0, 0.0, ALU.mult, ALU.add).then_inc(S["mask_set"], 1)

                def scale(n, which):
                    a, r = "12"[which], n % 2
                    ge("bn" + a, n)
                    pool.nop(nofuse=True)
                    g_.tensor_scalar(nmean[:, which, r:r + 1], mv[:, which, r, 0:1], -1.0, 0.0, ALU.mult, ALU.add)
                    g_.tensor_scalar(vare[:, which, r:r + 1], mv[:, which, r, 1:2], EPS, 1.0, ALU.add, ALU.mult)\
                        .then_inc(S[f"ln{a}a"], 1)
                    ge(f"ln{a}a", n)
                    g_.tensor_tensor(rstd[:, which, r:r + 1], vare[:, which, r:r + 1], half[:, :], ALU.pow)\
                        .then_inc(S[f"ln{a}b"], 1)

                def apply(n, which):
                    a, r = "12"[which], n % 2
                    ge(f"ln{a}b", n)
                    ge("lo" + a, n - 2)
                    pool.nop(nofuse=True)
                    g_.tensor_scalar(xn[:, which, r, :], stream(n, which), nmean[:, which, r:r + 1],
                                     rstd[:, which, r:r + 1], ALU.add, ALU.mult).then_inc(S["ln" + a], 1)
                    if which == 0:
                        ge("tr1", n - 2)
                        pool.nop(nofuse=True)
                        g_.tensor_scalar(xs[:, 0, r, 0, :], stream(n, 0), nmean[:, 0, r:r + 1], rstd[:, 0, r:r + 1],
                                         ALU.add, ALU.mult).then_inc(S["hi1"], 1)

                def add_bias(n, which):
                    bias = (b_proj, b_fc2)[which][visit(n)[0]]
                    g_.tensor_tensor(stream(n, which), stream(n, which), bias[:, :], ALU.add)\
                        .then_inc(S["bias" + "12"[which]], 1)

                def o_norm(n):
                    ge("inv_done", n)
                    for dst, done in ((o_tok[:, n % 2, :], "o_norm"), (os[:, n % 2, 0, :], "o_hi")):
                        g_.tensor_tensor(dst.rearrange("p (h d) -> p h d", d=HD), o_raw[:, n % 2, :, 0:HD],
                                         o_inv[:, n % 2, :].unsqueeze(2).broadcast_to([128, HEADS, HD]), ALU.mult)\
                            .then_inc(S[done], 1)

                def o_lo(n):
                    ge("o_hi", n)
                    g_.tensor_tensor(os[:, n % 2, 1, :], o_tok[:, n % 2, :], os[:, n % 2, 0, :], ALU.subtract)\
                        .then_inc(S["o_lo"], 1)

                def norm1_lo(n):
                    ge("hi1", n)
                    g_.tensor_tensor(xs[:, 0, n % 2, 1, :], xn[:, 0, n % 2, :], xs[:, 0, n % 2, 0, :],
                                     ALU.subtract).then_inc(S["lo1"], 1)

                def hidden_hi(m):
                    u = p * HC + m
                    ge("gelu", u)
                    pool.nop(nofuse=True)
                    g_.tensor_scalar(hid16[:, 0, m, :], hid[:, u % 2, :], 1.0, 0.0, ALU.mult, ALU.add)\
                        .then_inc(S["h_hi"], 1)

                p, place = mlp_phase(s)
                hid_slot = p >= -1 and place == 0
                if live(s + 1):
                    set_mask(s + 1)
                if live(s - 4):
                    scale(s - 4, 1)
                    apply(s - 4, 1)
                    add_bias(s - 4, 1)
                if hid_slot:
                    hidden_hi(0)
                    hidden_hi(1)
                    if live(s + 2):
                        scale(s + 2, 0)
                    hidden_hi(2)
                    hidden_hi(3)
                    if live(s + 2):
                        apply(s + 2, 0)
                    hidden_hi(4)
                    if live(s + 2):
                        add_bias(s + 2, 0)
                    hidden_hi(5)
                elif live(s + 2):
                    scale(s + 2, 0)
                    apply(s + 2, 0)
                    add_bias(s + 2, 0)
                if live(s - 2):
                    o_norm(s - 2)
                if live(s + 2):
                    norm1_lo(s + 2)
                if live(s - 2):
                    o_lo(s - 2)
                if s in ORDERED:
                    order_tiles(it, s)

            run(pool, slot)


_BLOCKS = [
    {"wqkv": "L0_conv_qkv_w", "bqkv": "L0_conv_qkv_b", "wproj": "L0_conv_proj_w", "bproj": "L0_conv_proj_b",
     "g1": "L0_conv_norm1_g", "b1": "L0_conv_norm1_b", "g2": "L0_conv_norm2_g", "b2": "L0_conv_norm2_b",
     "wfc1": "L0_conv_fc1_w", "bfc1": "L0_conv_fc1_b", "wfc2": "L0_conv_fc2_w", "bfc2": "L0_conv_fc2_b"},
    {"wqkv": "L1_conv_w_qkv", "bqkv": "L1_conv_b_qkv", "wproj": "L1_conv_w_proj", "bproj": "L1_conv_b_proj",
     "g1": "L1_conv_gamma1", "b1": "L1_conv_beta1", "g2": "L1_conv_gamma2", "b2": "L1_conv_beta2",
     "wfc1": "L1_conv_w_fc1", "bfc1": "L1_conv_b_fc1", "wfc2": "L1_conv_w_fc2", "bfc2": "L1_conv_b_fc2"},
]


def _constants(np):
    ident = np.eye(128, dtype=np.float32)
    r, c = np.divmod(np.arange(WIN), WS)
    q_mask = np.zeros((TOK, REGIONS), np.float32)
    q_mask[np.arange(TOK), np.tile(2 * (r >= SHIFT) + (c >= SHIFT), 2)] = 1.0
    k_mask = np.zeros((TOK, KINDS + 1, REGIONS), np.float32)
    for kind in range(KINDS):
        for w in range(2):
            for region in range(REGIONS):
                apart = np.zeros(WIN, bool)
                if kind // 2:
                    apart |= (r >= SHIFT) != (region // 2)
                if kind % 2 and w == 1:
                    apart |= (c >= SHIFT) != (region % 2)
                k_mask[w * WIN:(w + 1) * WIN, kind, region] = np.where(apart, np.float32(-10.0), np.float32(0.0))
    return ident, q_mask, k_mask


def kernel(**inputs):
    import numpy as _np
    import concourse.bacc as _bacc
    from concourse import mybir as _mybir
    from concourse.bass_utils import run_bass_kernel_spmd as _run

    nc = _bacc.Bacc("TRN2", target_bir_lowering=False, num_devices=1)
    ident, q_mask, k_mask = _constants(_np)
    given = {k: inputs[k] for k in inputs} | {"const_ident": ident, "const_q_mask": q_mask, "const_k_mask": k_mask}
    arrays, args = {}, {}
    for name, a in given.items():
        a = _np.ascontiguousarray(a)
        arrays[f"in_{name}_dram"] = a
        args[name] = nc.dram_tensor(f"in_{name}_dram", a.shape, _mybir.dt.from_np(a.dtype), kind="ExternalInput").ap()
    out = nc.dram_tensor("out_0_dram", (IMAGES, C, SIDE, SIDE), _mybir.dt.float32, kind="ExternalOutput").ap()
    layers = [{k: args[v] for k, v in b.items()} for b in _BLOCKS]
    swin_program(nc, args["x"], layers, args["L0_conv_rel_bias"], args["const_ident"], args["const_q_mask"], args["const_k_mask"],
                 out)
    r = _run(nc, [arrays], core_ids=[0])
    return r.results[0]["out_0_dram"]
```
